# Optimizing a Trainium2 kernel written in Bass

```python
import numpy as np
import jax
import jax.numpy as jnp

def _softmax(x, axis=-1):
    return jax.nn.softmax(x, axis=axis)

def _gelu(x):
    return jax.nn.gelu(x, approximate=True)

def _silu(x):
    return jax.nn.silu(x)

def _sigmoid(x):
    return jax.nn.sigmoid(x)

def _layernorm(x, axis=-1, eps=1e-05):
    m = jnp.mean(x, axis=axis, keepdims=True)
    v = jnp.var(x, axis=axis, keepdims=True)
    return (x - m) / jnp.sqrt(v + eps)

def _scatter_add(tgt, idx, src, axis=0):
    return tgt.at[idx].add(src)

def _segment_sum(src, seg, n):
    return jax.ops.segment_sum(src, seg, n)
kernel_name = 'mk_prb_d2_jaxref_r8_f325ac'

def setup_inputs(seed: int=0):
    np.random.seed(seed)
    _w = jnp.asarray

    def _L0_attn_setup():
        import jax, jax.numpy as jnp
        import numpy as np
        import math
        D = 256
        H = 32
        HKV = 8
        HD = D // H
        ROPE_BASE = 10000.0

        def _rope_cache(T, hd, base=ROPE_BASE):
            theta = 1.0 / base ** (jnp.arange(0, hd, 2, dtype=jnp.float32) / hd)
            t = jnp.arange(T, dtype=jnp.float32)
            freqs = t[:, None] * theta[None, :]
            return (jnp.cos(freqs), jnp.sin(freqs))

        def _apply_rope(x, cos, sin):
            B, Hh, T, hd = x.shape
            x_ = x.reshape(B, Hh, T, hd // 2, 2)
            x1, x2 = (x_[..., 0], x_[..., 1])
            c = cos[None, None, :, :]
            s = sin[None, None, :, :]
            rx1 = x1 * c - x2 * s
            rx2 = x1 * s + x2 * c
            return jnp.stack([rx1, rx2], axis=-1).reshape(B, Hh, T, hd)
        key = jax.random.key(seed)
        ks = jax.random.split(key, 5)
        B, T = (1, 256)
        sc = 0.02
        return {'x': jax.random.normal(ks[0], (B, T, D), dtype=jnp.float32), 'wq': jax.random.normal(ks[1], (D, D), dtype=jnp.float32) * sc, 'wk': jax.random.normal(ks[2], (HKV * HD, D), dtype=jnp.float32) * sc, 'wv': jax.random.normal(ks[3], (HKV * HD, D), dtype=jnp.float32) * sc, 'wo': jax.random.normal(ks[4], (D, D), dtype=jnp.float32) * sc}
    _L0_attn_in = _L0_attn_setup()

    def _L0_ffn_setup():
        import jax, jax.numpy as jnp
        import numpy as np
        HIDDEN = 256
        INTER = 1024
        SCALE = 64.0

        def fwht(x):
            orig_shape = x.shape
            n = orig_shape[-1]
            x = x.reshape(-1, n)
            h = 1
            while h < n:
                x = x.reshape(-1, n // (2 * h), 2, h)
                a, b = (x[:, :, 0, :], x[:, :, 1, :])
                x = jnp.stack([a + b, a - b], axis=2).reshape(-1, n)
                h *= 2
            return (x / jnp.sqrt(jnp.asarray(n, x.dtype))).reshape(orig_shape)
        key = jax.random.key(seed)
        ks = jax.random.split(key, 8)
        inp = jax.random.normal(ks[0], (4, 256, HIDDEN), dtype=jnp.float32)
        SU_ug = jnp.where(jax.random.bernoulli(ks[1], 0.5, (HIDDEN,)), 1.0, -1.0).astype(jnp.float32)
        SU_dp = jnp.where(jax.random.bernoulli(ks[2], 0.5, (INTER,)), 1.0, -1.0).astype(jnp.float32)
        Wscale_ug = jax.random.uniform(ks[3], (2 * INTER,), jnp.float32, 0.5, 1.5)
        Wscale_dp = jax.random.uniform(ks[4], (HIDDEN,), jnp.float32, 0.5, 1.5)
        W_up = jax.random.normal(ks[5], (INTER, HIDDEN), dtype=jnp.float32) * 0.02
        W_gate = jax.random.normal(ks[6], (INTER, HIDDEN), dtype=jnp.float32) * 0.02
        W_down = jax.random.normal(ks[7], (HIDDEN, INTER), dtype=jnp.float32) * 0.02
        return {'input': inp, 'SU_ug': SU_ug, 'SU_dp': SU_dp, 'Wscale_ug': Wscale_ug, 'Wscale_dp': Wscale_dp, 'W_up': W_up, 'W_gate': W_gate, 'W_down': W_down}
    _L0_ffn_in = _L0_ffn_setup()

    def _L1_attn_setup():
        import jax, jax.numpy as jnp
        import numpy as np
        L, N, E, H = (256, 2, 256, 16)
        DH = E // H
        SCALE = DH ** (-0.5)
        key = jax.random.key(seed)
        k1, k2, k3 = jax.random.split(key, 3)
        x = jax.random.normal(k1, (L, N, E), dtype=jnp.float32)
        weight_qkv = jax.random.normal(k2, (3 * E, E), dtype=jnp.float32) * 0.02
        weight_out = jax.random.normal(k3, (E, E), dtype=jnp.float32) * 0.02
        return {'x': x, 'weight_qkv': weight_qkv, 'weight_out': weight_out}
    _L1_attn_in = _L1_attn_setup()

    def _L1_ffn_setup():
        import jax, jax.numpy as jnp
        import numpy as np
        HIDDEN = 256
        INTER = 176
        N_EXPERTS = 64
        TOP_K = 8
        N_GROUP = 8
        TOPK_GROUP = 4
        SCALE = 2.5
        BSZ, SEQ = (1, 128)

        def _route(x, gate_weight, e_bias):
            T = x.shape[0]
            logits = x @ gate_weight.T
            scores = jax.nn.sigmoid(logits)
            s4c = scores + e_bias[None, :]
            per_group = s4c.reshape(T, N_GROUP, N_EXPERTS // N_GROUP)
            group_scores = jax.lax.top_k(per_group, 2)[0].sum(-1)
            group_idx = jax.lax.top_k(group_scores, TOPK_GROUP)[1]
            group_mask = jax.nn.one_hot(group_idx, N_GROUP, dtype=s4c.dtype).sum(1)
            score_mask = jnp.repeat(group_mask, N_EXPERTS // N_GROUP, axis=1)
            tmp = jnp.where(score_mask > 0, s4c, 0.0)
            topk_idx = jax.lax.top_k(tmp, TOP_K)[1]
            topk_w = jnp.take_along_axis(scores, topk_idx, axis=1)
            topk_w = topk_w / (topk_w.sum(-1, keepdims=True) + 1e-20) * SCALE
            return (topk_idx, topk_w)

        def _moe_forward(hidden_states, gate_weight, e_bias, gate_proj, up_proj, down_proj):
            B, S, H = hidden_states.shape
            x = hidden_states.reshape(-1, H)
            T = x.shape[0]
            topk_idx, topk_w = _route(x, gate_weight, e_bias)
            w_full = jnp.zeros((T, N_EXPERTS), dtype=x.dtype)
            w_full = w_full.at[jnp.arange(T)[:, None], topk_idx].add(topk_w)

            def step(out, ws):
                wg, wu, wd, we = ws
                inter = jax.nn.silu(x @ wg.T) * (x @ wu.T)
                return (out + inter @ wd.T * we[:, None], None)
            out, _ = jax.lax.scan(step, jnp.zeros_like(x), (gate_proj, up_proj, down_proj, w_full.T))
            return out.reshape(B, S, H)
        key = jax.random.key(seed)
        ks = jax.random.split(key, 6)
        return {'hidden_states': jax.random.normal(ks[0], (BSZ, SEQ, HIDDEN), dtype=jnp.float32), 'gate_weight': jax.random.normal(ks[1], (N_EXPERTS, HIDDEN), dtype=jnp.float32) * 0.02, 'e_score_correction_bias': jnp.zeros((N_EXPERTS,), dtype=jnp.float32), 'gate_proj': jax.random.normal(ks[2], (N_EXPERTS, INTER, HIDDEN), dtype=jnp.float32) * 0.02, 'up_proj': jax.random.normal(ks[3], (N_EXPERTS, INTER, HIDDEN), dtype=jnp.float32) * 0.02, 'down_proj': jax.random.normal(ks[4], (N_EXPERTS, HIDDEN, INTER), dtype=jnp.float32) * 0.02}
    _L1_ffn_in = _L1_ffn_setup()
    _d = {'L0_attn_x': _L0_attn_in['x'], 'L0_attn_wq': _L0_attn_in['wq'], 'L0_attn_wk': _L0_attn_in['wk'], 'L0_attn_wv': _L0_attn_in['wv'], 'L0_attn_wo': _L0_attn_in['wo'], 'L0_ffn_SU_ug': _L0_ffn_in['SU_ug'], 'L0_ffn_SU_dp': _L0_ffn_in['SU_dp'], 'L0_ffn_Wscale_ug': _L0_ffn_in['Wscale_ug'], 'L0_ffn_Wscale_dp': _L0_ffn_in['Wscale_dp'], 'L0_ffn_W_up': _L0_ffn_in['W_up'], 'L0_ffn_W_gate': _L0_ffn_in['W_gate'], 'L0_ffn_W_down': _L0_ffn_in['W_down'], 'L1_attn_weight_qkv': _L1_attn_in['weight_qkv'], 'L1_attn_weight_out': _L1_attn_in['weight_out'], 'L1_ffn_gate_weight': _L1_ffn_in['gate_weight'], 'L1_ffn_e_score_correction_bias': _L1_ffn_in['e_score_correction_bias'], 'L1_ffn_gate_proj': _L1_ffn_in['gate_proj'], 'L1_ffn_up_proj': _L1_ffn_in['up_proj'], 'L1_ffn_down_proj': _L1_ffn_in['down_proj']}
    _x0 = _d['L0_attn_x']
    _d['L0_attn_x'] = jax.random.normal(jax.random.fold_in(jax.random.key(seed), 1), (4, 512, 256), dtype=_x0.dtype)
    del _x0
    return _d

def reference(L0_attn_x, L0_attn_wq, L0_attn_wk, L0_attn_wv, L0_attn_wo, L0_ffn_SU_ug, L0_ffn_SU_dp, L0_ffn_Wscale_ug, L0_ffn_Wscale_dp, L0_ffn_W_up, L0_ffn_W_gate, L0_ffn_W_down, L1_attn_weight_qkv, L1_attn_weight_out, L1_ffn_gate_weight, L1_ffn_e_score_correction_bias, L1_ffn_gate_proj, L1_ffn_up_proj, L1_ffn_down_proj):

    def _L0_attn_ref(x, wq, wk, wv, wo):
        import jax, jax.numpy as jnp
        import numpy as np
        import math
        D = 256
        H = 32
        HKV = 8
        HD = D // H
        ROPE_BASE = 10000.0

        def _rope_cache(T, hd, base=ROPE_BASE):
            theta = 1.0 / base ** (jnp.arange(0, hd, 2, dtype=jnp.float32) / hd)
            t = jnp.arange(T, dtype=jnp.float32)
            freqs = t[:, None] * theta[None, :]
            return (jnp.cos(freqs), jnp.sin(freqs))

        def _apply_rope(x, cos, sin):
            B, Hh, T, hd = x.shape
            x_ = x.reshape(B, Hh, T, hd // 2, 2)
            x1, x2 = (x_[..., 0], x_[..., 1])
            c = cos[None, None, :, :]
            s = sin[None, None, :, :]
            rx1 = x1 * c - x2 * s
            rx2 = x1 * s + x2 * c
            return jnp.stack([rx1, rx2], axis=-1).reshape(B, Hh, T, hd)
        B, T, _ = x.shape
        q = (x @ wq.T).reshape(B, T, H, HD).transpose(0, 2, 1, 3)
        k = (x @ wk.T).reshape(B, T, HKV, HD).transpose(0, 2, 1, 3)
        v = (x @ wv.T).reshape(B, T, HKV, HD).transpose(0, 2, 1, 3)
        cos, sin = _rope_cache(T, HD)
        q = _apply_rope(q, cos, sin)
        k = _apply_rope(k, cos, sin)
        rep = H // HKV
        k = jnp.repeat(k, rep, axis=1)
        v = jnp.repeat(v, rep, axis=1)
        scores = jnp.einsum('bhtd,bhsd->bhts', q, k) / math.sqrt(HD)
        mask = jnp.triu(jnp.full((T, T), -jnp.inf, dtype=scores.dtype), k=1)
        scores = scores + mask[None, None, :, :]
        attn = jax.nn.softmax(scores, axis=-1)
        y = jnp.einsum('bhts,bhsd->bhtd', attn, v)
        y = y.transpose(0, 2, 1, 3).reshape(B, T, D)
        return y @ wo.T

    def _L0_ffn_ref(input, SU_ug, SU_dp, Wscale_ug, Wscale_dp, W_up, W_gate, W_down):
        import jax, jax.numpy as jnp
        import numpy as np
        HIDDEN = 256
        INTER = 1024
        SCALE = 64.0

        def fwht(x):
            orig_shape = x.shape
            n = orig_shape[-1]
            x = x.reshape(-1, n)
            h = 1
            while h < n:
                x = x.reshape(-1, n // (2 * h), 2, h)
                a, b = (x[:, :, 0, :], x[:, :, 1, :])
                x = jnp.stack([a + b, a - b], axis=2).reshape(-1, n)
                h *= 2
            return (x / jnp.sqrt(jnp.asarray(n, x.dtype))).reshape(orig_shape)
        n = SU_ug.shape[0]
        x = input.reshape(-1, n)
        x = fwht(x * SU_ug) / SCALE
        x_up = x @ W_up.T * (Wscale_ug[:INTER] * SCALE)
        x_gate = x @ W_gate.T * (Wscale_ug[INTER:] * SCALE)
        x = jax.nn.silu(x_gate) * x_up
        x = fwht(x * SU_dp) / SCALE
        x = x @ W_down.T * (Wscale_dp * SCALE)
        return x.reshape(input.shape)

    def _L1_attn_ref(x, weight_qkv, weight_out):
        import jax, jax.numpy as jnp
        import numpy as np
        L, N, E, H = (256, 2, 256, 16)
        DH = E // H
        SCALE = DH ** (-0.5)
        l, n, e = x.shape
        h, dh = (H, DH)
        qkv = jnp.einsum('lne,fe->lnf', x, weight_qkv)
        q, k, v = jnp.split(qkv, 3, axis=-1)
        q = q.reshape(l, n, h, dh) * jnp.asarray(SCALE, x.dtype)
        k = k.reshape(l, n, h, dh)
        v = v.reshape(l, n, h, dh)
        attn = jnp.einsum('lnhd,mnhd->nhlm', q, k)
        causal = jnp.tril(jnp.ones((l, l), dtype=bool))
        attn = jnp.where(causal, attn, jnp.asarray(-jnp.inf, attn.dtype))
        attn = jax.nn.softmax(attn, axis=-1)
        out = jnp.einsum('nhlm,mnhd->lnhd', attn, v).reshape(l, n, e)
        return jnp.einsum('lne,fe->lnf', out, weight_out)

    def _L1_ffn_ref(hidden_states, gate_weight, e_score_correction_bias, gate_proj, up_proj, down_proj):
        import jax, jax.numpy as jnp
        import numpy as np
        HIDDEN = 256
        INTER = 176
        N_EXPERTS = 64
        TOP_K = 8
        N_GROUP = 8
        TOPK_GROUP = 4
        SCALE = 2.5
        BSZ, SEQ = (1, 128)

        def _route(x, gate_weight, e_bias):
            T = x.shape[0]
            logits = x @ gate_weight.T
            scores = jax.nn.sigmoid(logits)
            s4c = scores + e_bias[None, :]
            per_group = s4c.reshape(T, N_GROUP, N_EXPERTS // N_GROUP)
            group_scores = jax.lax.top_k(per_group, 2)[0].sum(-1)
            group_idx = jax.lax.top_k(group_scores, TOPK_GROUP)[1]
            group_mask = jax.nn.one_hot(group_idx, N_GROUP, dtype=s4c.dtype).sum(1)
            score_mask = jnp.repeat(group_mask, N_EXPERTS // N_GROUP, axis=1)
            tmp = jnp.where(score_mask > 0, s4c, 0.0)
            topk_idx = jax.lax.top_k(tmp, TOP_K)[1]
            topk_w = jnp.take_along_axis(scores, topk_idx, axis=1)
            topk_w = topk_w / (topk_w.sum(-1, keepdims=True) + 1e-20) * SCALE
            return (topk_idx, topk_w)

        def _moe_forward(hidden_states, gate_weight, e_bias, gate_proj, up_proj, down_proj):
            B, S, H = hidden_states.shape
            x = hidden_states.reshape(-1, H)
            T = x.shape[0]
            topk_idx, topk_w = _route(x, gate_weight, e_bias)
            w_full = jnp.zeros((T, N_EXPERTS), dtype=x.dtype)
            w_full = w_full.at[jnp.arange(T)[:, None], topk_idx].add(topk_w)

            def step(out, ws):
                wg, wu, wd, we = ws
                inter = jax.nn.silu(x @ wg.T) * (x @ wu.T)
                return (out + inter @ wd.T * we[:, None], None)
            out, _ = jax.lax.scan(step, jnp.zeros_like(x), (gate_proj, up_proj, down_proj, w_full.T))
            return out.reshape(B, S, H)
        return _moe_forward(hidden_states, gate_weight, e_score_correction_bias, gate_proj, up_proj, down_proj)
    x = L0_attn_x
    xn = _layernorm(x, axis=-1)
    x = x + _L0_attn_ref(xn, L0_attn_wq, L0_attn_wk, L0_attn_wv, L0_attn_wo) + _L0_ffn_ref(xn, L0_ffn_SU_ug, L0_ffn_SU_dp, L0_ffn_Wscale_ug, L0_ffn_Wscale_dp, L0_ffn_W_up, L0_ffn_W_gate, L0_ffn_W_down)
    xn = _layernorm(x, axis=-1)
    x = x + _L1_attn_ref(xn, L1_attn_weight_qkv, L1_attn_weight_out) + _L1_ffn_ref(xn, L1_ffn_gate_weight, L1_ffn_e_score_correction_bias, L1_ffn_gate_proj, L1_ffn_up_proj, L1_ffn_down_proj)
    return x

_drawn_inputs = setup_inputs


def setup_inputs(seed=0):
    import zlib

    import numpy as np

    out = dict(_drawn_inputs(seed))
    spreads = {'L1_ffn_e_score_correction_bias': (0.0, 0.624)}
    factors = {'L0_attn_wq': 8.0,
     'L0_attn_wk': 8.0,
     'L0_attn_wv': 4.647,
     'L0_attn_wo': 4.618,
     'L0_ffn_Wscale_ug': 3.944,
     'L0_ffn_Wscale_dp': 5.478,
     'L1_ffn_gate_weight': 5.542,
     'L1_ffn_gate_proj': 4.596,
     'L1_ffn_up_proj': 4.554,
     'L1_ffn_down_proj': 4.549,
     'L1_attn_weight_qkv': 3.491,
     'L1_attn_weight_out': 3.491}
    for name, (base, spread) in spreads.items():
        noise = np.random.default_rng([zlib.crc32(name.encode()), seed]).standard_normal(out[name].shape)
        drawn = base * np.exp(spread * noise) if base else spread * noise
        out[name] = jnp.asarray(drawn.astype(out[name].dtype))
    for name, factor in factors.items():
        out[name] = (out[name] * factor).astype(out[name].dtype)
    return out
```

```python
import numpy as np
from contextlib import ExitStack
import concourse.bass as bass
from concourse import mybir

F32 = mybir.dt.float32
BF16 = mybir.dt.bfloat16
FP16 = mybir.dt.float16
U32 = mybir.dt.uint32
I32 = mybir.dt.int32
ALU = mybir.AluOpType
ACT = mybir.ActivationFunctionType
AX = mybir.AxisListType

P = 128
B, T, D = 4, 512, 256
TOK = B * T
NT = TOK // P
TPB = T // P
KD = D // P
EPS = 1e-5

H0, HKV, HD = 32, 8, 8
REP = H0 // HKV
QK = H0 * HD + HKV * HD
QKV = QK + HKV * HD
SCALE0 = HD ** -0.5
NP_ = 3
NC_ = NP_ * NP_
SROWS = 96
MROW = NC_ * HD
VW = 32

INTER0 = 1024
NI0 = INTER0 // P

H1, DH1 = 16, 16
SCALE1 = DH1 ** -0.5

NE, TOPK, NG, TOPG = 64, 8, 8, 4
EPG = NE // NG
INTER1 = 176
HI1 = INTER1 // 2
RSCALE = 2.5
NBLK = (TOK * TOPK + NE * (P - 1)) // P + 1
NBLK += NBLK % 2


SCRATCH = {
    "qk_parts": ((B, NP_ * 2 + 2, P, T), BF16),
    "xn1": ((NT, P, D), F32),
    "blocks": ((2 * P,), I32),
    "slots": ((NBLK, P, D), F32),
}


def sbuf(ctx, nc, name, shape, dt=F32):
    return ctx.enter_context(nc.sbuf_tensor(name, shape, dt))


def psum(ctx, nc, name, shape, dt=F32):
    return ctx.enter_context(nc.psum_tensor(name, shape, dt))


def sems(ctx, nc, *names):
    return [ctx.enter_context(nc.semaphore(n)) for n in names]


def prime(eng, *semaphores):
    for s in semaphores:
        eng.sem_inc(s, 1)


def apart(eng, sem):
    eng.sem_inc(sem, 1)


class Chain:

    def __init__(self, eng, sem):
        self.eng, self.sem, self.base, self.n = eng, sem, 0, 0

    def did(self, ins):
        ins.then_inc(self.sem, 1)
        self.n += 1

    def last(self):
        self.eng.wait_ge(self.sem, self.base + self.n)

    def step(self, ins):
        self.did(ins)
        self.last()

    def enter(self, i, per):
        self.start = self.n
        self.base = i * per

    def leave(self, count, per):
        assert self.n - self.start == per, (self.n - self.start, per)
        self.base, self.n = 0, self.start + count * per


def layer0_dense(nc, t, x_sb, v_pad):
    ctx = ExitStack()
    with ctx:
        ident = sbuf(ctx, nc, "a_ident", [P, P])
        identb = sbuf(ctx, nc, "a_identb", [P, P], BF16)
        had = sbuf(ctx, nc, "a_had", [P, 3, P])
        w_qkv = sbuf(ctx, nc, "a_w_qkv", [P, KD, QKV])
        rope = sbuf(ctx, nc, "a_rope", [P, TPB, 2, HD])
        w_raw = sbuf(ctx, nc, "a_w_raw", [P, KD, 2, INTER0])
        w_gu = sbuf(ctx, nc, "a_w_gu", [P, KD, 2, INTER0])
        wd_raw = sbuf(ctx, nc, "a_wd_raw", [P, NI0, D])
        wd_a = sbuf(ctx, nc, "a_wd_a", [P, NI0, D])
        wd_b = sbuf(ctx, nc, "a_wd_b", [P, NI0, D])
        w_down = sbuf(ctx, nc, "a_w_down", [P, NI0, D])
        su_ug = sbuf(ctx, nc, "a_su_ug", [P, KD])
        su_dp = sbuf(ctx, nc, "a_su_dp", [P, NI0])
        ws_ug = sbuf(ctx, nc, "a_ws_ug", [P, 2, NI0])
        ws_dp = sbuf(ctx, nc, "a_ws_dp", [P, D])
        stats = sbuf(ctx, nc, "a_stats", [P, TPB, 6])
        mv = sbuf(ctx, nc, "a_mv", [P, TPB, 2])
        var = sbuf(ctx, nc, "a_var", [P, TPB])
        std = sbuf(ctx, nc, "a_std", [P, TPB])
        rstd = sbuf(ctx, nc, "a_rstd", [P, TPB])
        xn = sbuf(ctx, nc, "a_xn", [P, TPB, D])
        xnT = sbuf(ctx, nc, "a_xnT", [P, KD, T])
        qk = sbuf(ctx, nc, "a_qk", [P, TPB, QK])
        rot = sbuf(ctx, nc, "a_rot", [P, QK])
        rot_b = sbuf(ctx, nc, "a_rot_b", [P, QK])
        rest = sbuf(ctx, nc, "a_rest", [P, QK])
        parts_q = sbuf(ctx, nc, "a_parts_q", [P, 2, NP_, H0 * HD], BF16)
        parts_k = sbuf(ctx, nc, "a_parts_k", [P, 2, NP_, HKV * HD], BF16)
        stage = sbuf(ctx, nc, "a_stage", [P, NP_ * 2 + 2, T], BF16)
        sg = sbuf(ctx, nc, "a_sg", [P, 2, T])
        hT = sbuf(ctx, nc, "a_hT", [P, NI0, T])

        ps_gu = psum(ctx, nc, "a_ps_gu", [P, 4, 512])
        ps_x = psum(ctx, nc, "a_ps_x", [P, 2, 512])
        ps_qkv = psum(ctx, nc, "a_ps_qkv", [P, 512])
        ps_parts = psum(ctx, nc, "a_ps_parts", [P, 8, P], BF16)

        (const_in, had_in, wgu_in, wd_in, wqkv_in, scale_in, dve_step, had_ready, had_copied,
         down_had, down_copied, var_ready, std_ready, xn_ready, xT_ready, xT_copied,
         qkv_ready, qkv_copied, parts_ready, partsT_ready, partsT_copied, stored, gu_ready,
         silu_ready, h_ready, down_ready, added, w_ready, v_clear, waits) = sems(
            ctx, nc, *("a_" + s for s in (
                "const_in had_in wgu_in wd_in wqkv_in scale_in dve_step had_ready had_copied "
                "down_had down_copied var_ready std_ready xn_ready xT_ready xT_copied "
                "qkv_ready qkv_copied parts_ready partsT_ready partsT_copied stored gu_ready "
                "silu_ready h_ready down_ready added w_ready v_clear waits").split()))
        x_in = sems(ctx, nc, *(f"a_x_in{b}" for b in range(B)))
        block = ctx.enter_context(nc.Block())

        @block.sync
        def _(sp):
            prime(sp, stored)
            sp.dma_start(had[:, :, :], t["had"]).then_inc(had_in, 16)
            for m, name in enumerate(("w_gateT", "w_upT")):
                sp.dma_start(w_raw[:, :, m, :],
                             t[name].rearrange("(k p) i -> p k i", p=P)).then_inc(wgu_in, 16)
            sp.dma_start(wd_raw[:, :, :], t["w_downT"].rearrange("(j p) d -> p j d", p=P))\
              .then_inc(wd_in, 16)
            with sp.Fori(0, B) as n:
                sp.wait_ge(partsT_copied, 1 + (n + 1) * TPB)
                sp.dma_start(t["qk_parts"][bass.ds(n, 1)].rearrange("b m p s -> p (b m) s"),
                             stage[:, :, :]).then_inc(stored, 16)
            sp.wait_ge(stored, 1 + B * 16)

        @block.gpsimd
        def _(pool):
            pool.memset(v_pad[:, :, :, :], 0.0).then_inc(v_clear, 1)
            pool.wait_ge(v_clear, 1)
            pool.memset(v_pad[:, :, :, HD:HD + 1], 1.0).then_inc(v_clear, 1)

        @block.scalar
        def _(act):
            prime(act, qkv_copied, partsT_copied)
            act.dma_start(su_ug[:, :], t["su_ug"].rearrange("(k p) -> p k", p=P),
                          allow_slow_non_contiguous=True).then_inc(scale_in, 16)
            act.dma_start(su_dp[:, :], t["su_dp"].rearrange("(k p) -> p k", p=P),
                          allow_slow_non_contiguous=True).then_inc(scale_in, 16)
            act.dma_start(ws_ug[:, :, :], t["ws_ug"].rearrange("(m i p) -> p m i", p=P, m=2),
                          allow_slow_non_contiguous=True).then_inc(scale_in, 16)
            act.dma_start(ws_dp[:, :], t["ws_dp"].partition_broadcast(P)).then_inc(scale_in, 16)
            for b in range(B):
                act.dma_start(x_sb[:, TPB * b:TPB * (b + 1), :],
                              t["x"][T * b:T * (b + 1), :].rearrange("(i p) d -> p i d", p=P))\
                   .then_inc(x_in[b], 16)
            act.dma_start(ident[:, :], t["ident"]).then_inc(const_in, 16)
            act.dma_start(identb[:, :], t["identb"]).then_inc(const_in, 16)
            act.dma_start(rope[:, :, :, :], t["rope"]).then_inc(const_in, 16)
            for c0, c1, name in ((0, H0 * HD, "wqT"), (H0 * HD, QK, "wkT"), (QK, QKV, "wvT")):
                act.dma_start(w_qkv[:, :, c0:c1],
                              t[name].rearrange("(k p) i -> p k i", p=P)).then_inc(wqkv_in, 16)
            act.wait_ge(scale_in, 64)
            for m in range(KD):
                for w in range(2):
                    for c in range(2):
                        s = (m * 2 + w) * 2 + c
                        act.wait_ge(had_ready, s + 1)
                        nc.scalar.activation(w_gu[:, m, w, c * 512:(c + 1) * 512], ps_gu[:, s % 4, :],
                                             ACT.Copy, scale=su_ug[:, m:m + 1]).then_inc(had_copied, 1)
            act.wait_ge(down_had, 1)
            nc.scalar.activation(wd_a[:, :, :].rearrange("p (c a) d -> p c (a d)", c=4),
                                 ps_gu[:, :, :], ACT.Copy).then_inc(down_copied, 1)
            act.wait_ge(v_clear, 2)
            with act.Fori(0, B) as n:
                act.wait_ge(var_ready, n + 1)
                nc.scalar.activation(std[:, :], var[:, :], ACT.Sqrt).then_inc(std_ready, 1)
                act.wait_ge(gu_ready, 1 + n * NI0)
                for i in range(TPB):
                    act.wait_ge(xT_ready, 1 + n * TPB + i + 1)
                    nc.scalar.activation(xnT[:, :, i * P:(i + 1) * P],
                                         ps_x[:, i % 2, 0:D].rearrange("p (k c) -> p k c", k=KD),
                                         ACT.Copy).then_inc(xT_copied, 1)
                act.wait_ge(parts_ready, 1 + n * TPB * 2)
                for i in range(TPB):
                    act.wait_ge(qkv_ready, n * TPB + i + 1)
                    nc.scalar.activation(qk[:, i, :], ps_qkv[:, 0:QK], ACT.Copy).then_inc(qkv_copied, 1)
                    nc.scalar.activation(
                        v_pad[:, bass.ds(n * TPB + i, 1), :, 0:HD].rearrange("p a g d -> p (a g) d"),
                        ps_qkv[:, QK:QKV].rearrange("p (g d) -> p g d", d=HD),
                        ACT.Copy).then_inc(qkv_copied, 1)

                def copy_parts(i):
                    act.wait_ge(partsT_ready, 1 + n * TPB + i + 1)
                    nc.scalar.activation(stage[:, :, i * P:(i + 1) * P], ps_parts[:, :, :],
                                         ACT.Copy).then_inc(partsT_copied, 1)

                for i in range(NI0):
                    act.wait_ge(gu_ready, 1 + n * NI0 + i + 1)
                    if i >= 2:
                        act.wait_ge(h_ready, 1 + n * NI0 + i - 1)
                    else:
                        act.wait_ge(h_ready, 1 + n * NI0)
                    nc.scalar.activation(sg[:, i % 2, :], ps_gu[:, 2 * (i % 2), :], ACT.Silu,
                                         scale=ws_ug[:, 1, i:i + 1]).then_inc(silu_ready, 1)
                    if i == 0:
                        act.wait_ge(stored, 1 + n * 16)
                    if 1 <= i <= TPB:
                        copy_parts(i - 1)

        @block.vector
        def _(dve):
            prime(dve, parts_ready, h_ready, added)
            ch = Chain(dve, dve_step)
            dve.wait_ge(down_copied, 1)
            src, dst = wd_a, wd_b
            for h in (1, 2, 4):
                a = src[:, :, :].rearrange("p (u r h) d -> p u r (h d)", r=2, h=h)
                o = dst[:, :, :].rearrange("p (u r h) d -> p u r (h d)", r=2, h=h)
                ch.did(nc.vector.tensor_tensor(o[:, :, 0, :], a[:, :, 0, :], a[:, :, 1, :], ALU.add))
                ch.step(nc.vector.tensor_tensor(o[:, :, 1, :], a[:, :, 0, :], a[:, :, 1, :], ALU.subtract))
                src, dst = dst, src
            dve.wait_ge(scale_in, 64)
            for j in range(NI0):
                ins = nc.vector.scalar_tensor_tensor(w_down[:, j, :], src[:, j, :], su_dp[:, j:j + 1],
                                                     ws_dp[:, :], ALU.mult, ALU.mult)
            ins.then_inc(w_ready, 1)
            for b in range(B):
                dve.wait_ge(x_in[b], 16)
            dve.wait_ge(const_in, 48)
            PER = 2 * TPB + 1 + TPB * 10
            with dve.Fori(0, B) as n:
                ch.enter(n, PER)
                apart(dve, waits)
                for i in range(TPB):
                    xi = x_sb[:, bass.ds(n * TPB + i, 1), :].rearrange("p a d -> p (a d)")
                    ch.did(nc.vector.bn_stats(stats[:, i, :], xi))
                ch.last()
                apart(dve, waits)
                for i in range(TPB):
                    ch.did(nc.vector.bn_aggr(mv[:, i, :], stats[:, i, :]))
                ch.last()
                nc.vector.tensor_scalar(var[:, :], mv[:, :, 1], EPS, None, ALU.add).then_inc(var_ready, 1)
                dve.wait_ge(std_ready, n + 1)
                ch.step(nc.vector.reciprocal(rstd[:, :], std[:, :]))
                dve.wait_ge(xT_ready, 1 + n * TPB)
                for i in range(TPB):
                    xi = x_sb[:, bass.ds(n * TPB + i, 1), :].rearrange("p a d -> p (a d)")
                    nc.vector.tensor_scalar(xn[:, i, :], xi, mv[:, i, 0:1], rstd[:, i:i + 1],
                                            ALU.subtract, ALU.mult).then_inc(xn_ready, 1)

                def rotate(i):
                    dve.wait_ge(qkv_copied, 1 + (n * TPB + i + 1) * 2)
                    q3 = qk[:, i, :].rearrange("p (h c) -> p h c", c=HD)
                    q4 = qk[:, i, :].rearrange("p (h c r) -> p h c r", c=HD // 2, r=2)
                    b4 = rot_b[:, :].rearrange("p (h c r) -> p h c r", c=HD // 2, r=2)
                    cos = rope[:, i, 0:1, :].to_broadcast([P, QK // HD, HD])
                    sin = rope[:, i, 1:2, :].rearrange("p a (c r) -> p a c r", r=2)
                    ch.did(nc.vector.tensor_tensor(rot[:, :].rearrange("p (h c) -> p h c", c=HD),
                                                   q3, cos, ALU.mult))
                    for r in range(2):
                        ch.did(nc.vector.tensor_tensor(
                            b4[:, :, :, r], q4[:, :, :, 1 - r],
                            sin[:, :, :, r].to_broadcast([P, QK // HD, HD // 2]), ALU.mult))
                    ch.last()
                    ch.step(nc.vector.tensor_tensor(rot[:, :], rot[:, :], rot_b[:, :], ALU.add))
                    if i >= 2:
                        dve.wait_ge(partsT_ready, 1 + n * TPB + i - 1)
                    else:
                        dve.wait_ge(partsT_ready, 1 + n * TPB)
                    pq, pk = parts_q[:, i % 2], parts_k[:, i % 2]
                    nq = H0 * HD
                    ch.did(nc.vector.tensor_copy(pq[:, 0, :], rot[:, 0:nq]))
                    ch.step(nc.vector.tensor_copy(pk[:, 0, :], rot[:, nq:]))
                    ch.did(nc.vector.tensor_tensor(rest[:, 0:nq], rot[:, 0:nq], pq[:, 0, :], ALU.subtract))
                    ch.step(nc.vector.tensor_tensor(rest[:, nq:], rot[:, nq:], pk[:, 0, :], ALU.subtract))
                    ch.did(nc.vector.tensor_copy(pq[:, 1, :], rest[:, 0:nq]))
                    ch.step(nc.vector.tensor_copy(pk[:, 1, :], rest[:, nq:]))
                    nc.vector.tensor_tensor(pq[:, 2, :], rest[:, 0:nq], pq[:, 1, :], ALU.subtract)\
                      .then_inc(parts_ready, 1)
                    nc.vector.tensor_tensor(pk[:, 2, :], rest[:, nq:], pk[:, 1, :], ALU.subtract)\
                      .then_inc(parts_ready, 1)

                def gate(i):
                    dve.wait_ge(silu_ready, n * NI0 + i + 1)
                    if i == 0:
                        dve.wait_ge(down_ready, 1 + n * TPB)
                    nc.vector.scalar_tensor_tensor(hT[:, i, :], ps_gu[:, 2 * (i % 2) + 1, :],
                                                   ws_ug[:, 0, i:i + 1], sg[:, i % 2, :],
                                                   ALU.mult, ALU.mult).then_inc(h_ready, 1)

                rotate(0)
                rotate(1)
                gate(0)
                rotate(2)
                gate(1)
                rotate(3)
                for i in range(2, NI0):
                    gate(i)
                for i in range(TPB):
                    xi = x_sb[:, bass.ds(n * TPB + i, 1), :].rearrange("p a d -> p (a d)")
                    dve.wait_ge(down_ready, 1 + n * TPB + i + 1)
                    nc.vector.tensor_tensor(xi, xi, ps_x[:, i % 2, 0:D], ALU.add).then_inc(added, 1)
                dve.wait_ge(added, 1 + (n + 1) * TPB)
                ch.leave(B, PER)

        @block.tensor
        def _(pe):
            prime(pe, gu_ready, xT_ready, partsT_ready, down_ready)
            pe.wait_ge(had_in, 16)
            pe.wait_ge(wgu_in, 32)
            for m in range(KD):
                for w in range(2):
                    for c in range(2):
                        s = (m * 2 + w) * 2 + c
                        if s >= 4:
                            pe.wait_ge(had_copied, s - 3)
                        for k in range(KD):
                            ins = nc.tensor.matmul(ps_gu[:, s % 4, :], had[:, m & k, :],
                                                   w_raw[:, k, w, c * 512:(c + 1) * 512],
                                                   start=(k == 0), stop=(k == KD - 1))
                        ins.then_inc(had_ready, 1)
            pe.wait_ge(wd_in, 16)
            pe.wait_ge(had_copied, 8)
            wd = wd_raw[:, :, :].rearrange("p (c a) d -> p c (a d)", c=4)
            for c in range(4):
                ins = nc.tensor.matmul(ps_gu[:, c, :], had[:, 2, :], wd[:, c, :], start=True, stop=True)
            ins.then_inc(down_had, 1)
            pe.wait_ge(down_copied, 1)
            pe.wait_ge(const_in, 48)
            pe.wait_ge(wqkv_in, 48)
            with pe.Fori(0, B) as n:
                pe.wait_ge(added, 1 + n * TPB)
                for i in range(TPB):
                    pe.wait_ge(xn_ready, n * TPB + i + 1)
                    if i >= 2:
                        pe.wait_ge(xT_copied, n * TPB + i - 1)
                    for k in range(KD):
                        ins = nc.tensor.transpose(ps_x[:, i % 2, k * P:(k + 1) * P],
                                                  xn[:, i, k * P:(k + 1) * P], ident[:, :])
                    ins.then_inc(xT_ready, 1)
                for i in range(TPB):
                    pe.wait_ge(xT_copied, n * TPB + i + 1)
                    pe.wait_ge(qkv_copied, 1 + (n * TPB + i) * 2)
                    for k in range(KD):
                        ins = nc.tensor.matmul(ps_qkv[:, 0:QKV], xnT[:, k, i * P:(i + 1) * P],
                                               w_qkv[:, k, :], start=(k == 0), stop=(k == KD - 1))
                    ins.then_inc(qkv_ready, 1)

                def parts_T(i):
                    pe.wait_ge(parts_ready, 1 + (n * TPB + i + 1) * 2)
                    pe.wait_ge(partsT_copied, 1 + n * TPB + i)
                    for s in range(NP_):
                        for m in range(2):
                            nc.tensor.transpose(ps_parts[:, s * 2 + m, :],
                                                parts_q[:, i % 2, s, m * P:(m + 1) * P], identb[:, :])
                    for s in range(2):
                        ins = nc.tensor.transpose(
                            ps_parts[:, NP_ * 2 + s, :],
                            parts_k[:, i % 2, s:s + 2, :].rearrange("p s c -> p (s c)"), identb[:, :])
                    ins.then_inc(partsT_ready, 1)

                for i in range(NI0):
                    if i >= 2:
                        pe.wait_ge(h_ready, 1 + n * NI0 + i - 1)
                    else:
                        pe.wait_ge(h_ready, 1 + n * NI0)
                    for w in range(2):
                        for k in range(KD):
                            ins = nc.tensor.matmul(ps_gu[:, 2 * (i % 2) + w, :],
                                                   w_gu[:, k, w, i * P:(i + 1) * P], xnT[:, k, :],
                                                   start=(k == 0), stop=(k == KD - 1))
                    ins.then_inc(gu_ready, 1)
                    if 1 <= i <= TPB:
                        parts_T(i - 1)
                pe.wait_ge(w_ready, 1)
                pe.wait_ge(h_ready, 1 + (n + 1) * NI0)
                for i in range(TPB):
                    if i >= 2:
                        pe.wait_ge(added, 1 + n * TPB + i - 1)
                    for k in range(NI0):
                        ins = nc.tensor.matmul(ps_x[:, i % 2, 0:D], hT[:, k, i * P:(i + 1) * P],
                                               w_down[:, k, :], start=(k == 0), stop=(k == NI0 - 1))
                    ins.then_inc(down_ready, 1)


def layer0_attention(nc, t, v_pad, yn):
    ctx = ExitStack()
    with ctx:
        ident = sbuf(ctx, nc, "b_ident", [P, P])
        identb = sbuf(ctx, nc, "b_identb", [P, P], BF16)
        causal = sbuf(ctx, nc, "b_causal", [P, 2, P], BF16)
        qT = [sbuf(ctx, nc, f"b_qT{i}", [SROWS, HKV, REP, T], BF16) for i in range(2)]
        kT = [sbuf(ctx, nc, f"b_kT{i}", [SROWS, HKV, T], BF16) for i in range(2)]
        negmax = sbuf(ctx, nc, "b_negmax", [P, HKV, REP, TPB])
        negmaxT = sbuf(ctx, nc, "b_negmaxT", [P, P])
        m_rest = sbuf(ctx, nc, "b_m_rest", [P, P])
        m_parts = sbuf(ctx, nc, "b_m_parts", [P, NP_, P], BF16)
        probs = sbuf(ctx, nc, "b_probs", [P, 2, 1280])
        y_raw = sbuf(ctx, nc, "b_y_raw", [P, 2, T])
        rden = sbuf(ctx, nc, "b_rden", [P, TPB, 4])

        ps_s = psum(ctx, nc, "b_ps_s", [P, 2, 512])
        ps_e = psum(ctx, nc, "b_ps_e", [P, 3, 512])
        ps_y = psum(ctx, nc, "b_ps_y", [P, 2, 512])
        ps_t = psum(ctx, nc, "b_ps_t", [P, TPB, P])

        (const_in, step, max_ready, max_done, heads_done, mT_ready, m_split, m_in,
         st_ready, exp_done, pv_done, y_copied, yT_ready, norm_done) = sems(
            ctx, nc, *("b_" + s for s in (
                "const_in step max_ready max_done heads_done mT_ready m_split m_in "
                "st_ready exp_done pv_done y_copied yT_ready norm_done").split()))
        loaded = sems(ctx, nc, "b_loaded0", "b_loaded1")
        block = ctx.enter_context(nc.Block())
        NLOAD = 2 * NC_ + 2
        UNITS = [[(0, 0)], [(3, 0), (1, P)], [(2, 0)]]
        UCOL = [0, 512, 1024, 1280]
        MUNITS = [[(3, 0)], [(2, 0), (0, 3 * P)], [(1, 0)]]

        @block.sync
        def _(sp):
            sp.dma_start(ident[:, :], t["ident"]).then_inc(const_in, 16)
            sp.dma_start(identb[:, :], t["identb"]).then_inc(const_in, 16)
            sp.dma_start(causal[:, :, :], t["causal"]).then_inc(const_in, 16)
            for b in range(B + 1):
                if b < B:
                    q, k, sem = qT[b % 2], kT[b % 2], loaded[b % 2]
                    if b >= 2:
                        sp.wait_ge(pv_done, 1 + (b - 1) * REP * HKV)
                    sp.dma_start(q[MROW:SROWS].rearrange("p g r s -> p (g r) s"),
                                 t["pad"][0:1].rearrange("a p s -> p a s")
                                 .to_broadcast([SROWS - MROW, H0, T])).then_inc(sem, 16)
                    sp.dma_start(k[MROW:SROWS],
                                 t["pad"][1:2].rearrange("a p s -> p a s")
                                 .to_broadcast([SROWS - MROW, HKV, T])).then_inc(sem, 16)
                    for i in range(NP_):
                        for j in range(NP_):
                            r = (i * NP_ + j) * HD
                            sp.dma_start(q[r:r + HD].rearrange("p g r s -> p (g r) s"),
                                         t["qk_parts"][b, 2 * i:2 * i + 2]
                                         .rearrange("m (h d) s -> d (m h) s", d=HD)).then_inc(sem, 16)
                            slot, row = ((6, 0), (7, 0), (7, 64))[j]
                            sp.dma_start(k[r:r + HD],
                                         t["qk_parts"][b, slot, row:row + HKV * HD]
                                         .rearrange("(h d) s -> d h s", d=HD)).then_inc(sem, 16)
                if b >= 1:
                    sp.wait_ge(m_split, b)
                    for s in range(NP_):
                        sp.dma_start(qT[(b - 1) % 2][MROW + s:MROW + s + 1]
                                     .rearrange("p g r s -> p (g r s)"),
                                     m_parts[:, s, :]).then_inc(m_in, 16)

        @block.scalar
        def _(act):
            prime(act, exp_done, y_copied)
            for b in range(B):
                with act.Fori(0, REP) as h:
                    hi = h + b * REP

                    def copy_y(G):
                        act.wait_ge(pv_done, 1 + hi * HKV + 4 * G + 4)
                        act.wait_ge(yT_ready, 1 + hi * 2)
                        nc.scalar.activation(y_raw[:, G, :], ps_y[:, G, :], ACT.Copy).then_inc(y_copied, 1)

                    for g in range(HKV):
                        gi = hi * HKV + g
                        act.wait_ge(pv_done, 1 + (gi - 1 if g >= 2 else hi * HKV))
                        for u in range(3):
                            act.wait_ge(st_ready, gi * 3 + u + 1)
                            n = UCOL[u + 1] - UCOL[u]
                            nc.scalar.activation(probs[:, g % 2, UCOL[u]:UCOL[u + 1]], ps_e[:, u, 0:n],
                                                 ACT.Exp, scale=SCALE0).then_inc(exp_done, 1)
                        if g == 4:
                            copy_y(0)
                    copy_y(1)

        @block.vector
        def _(dve):
            prime(dve, norm_done, max_done)
            for ph in range(B + 1):
                with dve.Fori(0, REP) as h:
                    hi = h + (ph - 1) * REP if ph else h

                    def normalize(G):
                        dve.wait_ge(yT_ready, 1 + hi * 2 + G + 1)
                        y = ps_t[:, :, :].rearrange("p a (j c) -> p a j c", c=VW)
                        nc.vector.reciprocal(rden[:, :, :], y[:, :, :, HD]).then_inc(step, 1)
                        dve.wait_ge(step, hi * 2 + G + 1)
                        b = ph - 1
                        o = yn[:, b * TPB:(b + 1) * TPB, :]\
                            .rearrange("p a (G j r d) -> p a G j r d", G=2, j=4, r=REP)
                        o = o[:, :, G, :, bass.ds(h, 1), :].rearrange("p a j r d -> p a j (r d)")
                        nc.vector.tensor_tensor(o, y[:, :, :, 0:HD],
                                                rden[:, :, :].rearrange("p a (j c) -> p a j c", c=1)
                                                .to_broadcast([P, TPB, 4, HD]),
                                                ALU.mult).then_inc(norm_done, 1)

                    for g in range(HKV):
                        if ph < B:
                            gi = (h + ph * REP) * HKV + g
                            for u in range(3):
                                dve.wait_ge(max_ready, gi * 3 + u + 1)
                                if g == 0 and u == 0 and ph >= 1:
                                    dve.wait_ge(mT_ready, ph)
                                for q, c in MUNITS[u]:
                                    ins = nc.vector.tensor_reduce(
                                        negmax[:, g, bass.ds(h, 1), q],
                                        ps_s[:, (3 * g + u) % 2, c:c + (q + 1) * P],
                                        AX.X, ALU.max, negate=True)
                                ins.then_inc(max_done, 1)
                        if ph and g == 6:
                            normalize(0)
                    if ph:
                        normalize(1)
                if ph < B:
                    dve.wait_ge(max_done, 1 + (ph + 1) * REP * HKV * 3)
                    dve.wait_ge(mT_ready, ph + 1)
                    base = ph * 5
                    nc.vector.tensor_copy(negmaxT[:, :], ps_t[:, 0, :]).then_inc(heads_done, 1)
                    dve.wait_ge(heads_done, base + 1)
                    if ph:
                        dve.wait_ge(m_in, ph * 48)
                    nc.vector.tensor_copy(m_parts[:, 0, :], negmaxT[:, :]).then_inc(heads_done, 1)
                    dve.wait_ge(heads_done, base + 2)
                    nc.vector.tensor_tensor(m_rest[:, :], negmaxT[:, :], m_parts[:, 0, :],
                                            ALU.subtract).then_inc(heads_done, 1)
                    dve.wait_ge(heads_done, base + 3)
                    nc.vector.tensor_copy(m_parts[:, 1, :], m_rest[:, :]).then_inc(heads_done, 1)
                    dve.wait_ge(heads_done, base + 4)
                    nc.vector.tensor_tensor(m_parts[:, 2, :], m_rest[:, :], m_parts[:, 1, :],
                                            ALU.subtract).then_inc(heads_done, 1)
                    dve.wait_ge(heads_done, base + 5)
                    nc.vector.engine_nop().then_inc(m_split, 1)

        @block.tensor
        def _(pe):
            prime(pe, pv_done, yT_ready)
            pe.wait_ge(const_in, 48)
            for ph in range(B + 1):
                if ph < B:
                    pe.wait_ge(loaded[ph % 2], NLOAD * 16 * (ph // 2 + 1))
                if ph:
                    pe.wait_ge(m_in, 48 * ph)
                with pe.Fori(0, REP) as h:
                    mi = h + ph * REP
                    hi = h + (ph - 1) * REP if ph else h

                    def head(x, g, c0, c1):
                        return x[:, g, bass.ds(h, 1), c0:c1].rearrange("p r s -> p (r s)")

                    def max_scores(g, u):
                        q, k = qT[ph % 2], kT[ph % 2]
                        n = 3 * g + u
                        pe.wait_ge(max_done, 1 + (mi * 3 * HKV + (n - 1 if n else 0)))
                        out = ps_s[:, n % 2, :]
                        for a, c in MUNITS[u]:
                            nc.tensor.matmul(out[:, c:c + (a + 1) * P], head(q, g, a * P, (a + 1) * P),
                                             k[:, g, 0:(a + 1) * P], start=True, stop=False,
                                             skip_group_check=True)
                            ins = nc.tensor.matmul(out[:, c + a * P:c + (a + 1) * P], identb[:, :],
                                                   causal[:, 0, :], start=False, stop=True,
                                                   skip_group_check=True)
                        ins.then_inc(max_ready, 1)

                    def key_scores(g):
                        q, k = qT[(ph - 1) % 2], kT[(ph - 1) % 2]
                        gi = hi * HKV + g
                        for u in range(3):
                            pe.wait_ge(exp_done, 1 + (gi * 3 + (u - 2 if g else 0)))
                            for s, c in UNITS[u]:
                                nc.tensor.matmul(ps_e[:, u, c:c + T - s * P],
                                                 k[:, g, s * P:(s + 1) * P], head(q, g, s * P, T),
                                                 start=True, stop=False, skip_group_check=True)
                                ins = nc.tensor.matmul(ps_e[:, u, c:c + P], identb[:, :],
                                                       causal[:, 1, :], start=False, stop=True,
                                                       skip_group_check=True)
                            ins.then_inc(st_ready, 1)

                    def values(g, u):
                        gi = hi * HKV + g
                        G, j = g // 4, g % 4
                        if u == 0 and j == 0:
                            pe.wait_ge(y_copied, 1 + hi * 2)
                        pe.wait_ge(exp_done, 1 + gi * 3 + u + 1)
                        for s, c in UNITS[u]:
                            ins = nc.tensor.matmul(
                                ps_y[VW * j:VW * (j + 1), G, s * P:T],
                                v_pad[:, (ph - 1) * TPB + s, g, :],
                                probs[:, g % 2, UCOL[u] + c:UCOL[u] + c + T - s * P],
                                start=(s == 0), stop=(u == 2), skip_group_check=True)
                        if u == 2:
                            ins.then_inc(pv_done, 1)

                    def transposes(G):
                        pe.wait_ge(y_copied, 1 + hi * 2 + G + 1)
                        pe.wait_ge(norm_done, 1 + hi * 2 + G)
                        for a in range(TPB):
                            ins = nc.tensor.transpose(ps_t[:, a, :], y_raw[:, G, a * P:(a + 1) * P],
                                                      ident[:, :])
                        ins.then_inc(yT_ready, 1)

                    for g in range(HKV):
                        if ph:
                            key_scores(g)
                        for u in range(3):
                            if ph < B:
                                max_scores(g, u)
                            if ph and g:
                                values(g - 1, u)
                        if ph and g == 6:
                            transposes(0)
                    if ph:
                        for u in range(3):
                            values(HKV - 1, u)
                        transposes(1)
                if ph < B:
                    pe.wait_ge(max_done, 1 + (ph + 1) * REP * HKV * 3)
                    if ph:
                        pe.wait_ge(norm_done, 1 + ph * REP * 2)
                    nc.tensor.transpose(ps_t[:, 0, :], negmax[:, :, :, :].rearrange("p g r a -> p (g r a)"),
                                        ident[:, :]).then_inc(mT_ready, 1)


def layer1_front(nc, t, x_sb, yn, qkv1, logits):
    ctx = ExitStack()
    with ctx:
        ident = sbuf(ctx, nc, "c_ident", [P, P])
        w_o = sbuf(ctx, nc, "c_w_o", [P, KD, D])
        w_r = sbuf(ctx, nc, "c_w_r", [P, KD, NE])
        w_qkv = sbuf(ctx, nc, "c_w_qkv", [P, KD, 3 * D])
        y_cur = sbuf(ctx, nc, "c_y_cur", [P, 2, D])
        yT = sbuf(ctx, nc, "c_yT", [P, 2, KD, P])
        xn = sbuf(ctx, nc, "c_xn", [P, 2, D])
        xT = sbuf(ctx, nc, "c_xT", [P, 2, KD, P])
        stats = sbuf(ctx, nc, "c_stats", [P, 6])
        mv = sbuf(ctx, nc, "c_mv", [P, 2])
        var = sbuf(ctx, nc, "c_var", [P, 1])
        std = sbuf(ctx, nc, "c_std", [P, 1])
        rstd = sbuf(ctx, nc, "c_rstd", [P, 1])

        ps_yT = psum(ctx, nc, "c_ps_yT", [P, 512])
        ps_o = psum(ctx, nc, "c_ps_o", [P, 512])
        ps_xT = psum(ctx, nc, "c_ps_xT", [P, 512])
        ps_r = psum(ctx, nc, "c_ps_r", [P, 512])
        ps_qkv = psum(ctx, nc, "c_ps_qkv", [P, 2, 2, 512])

        (w_in, step, y_ready, yT_ready, yT_copied, o_ready, var_ready, std_ready, xn_ready,
         xn_stored, xT_ready, xT_copied, r_ready, r_copied, qkv_ready, qkv_copied, waits) = sems(
            ctx, nc, *("c_" + s for s in (
                "w_in step y_ready yT_ready yT_copied o_ready var_ready std_ready xn_ready "
                "xn_stored xT_ready xT_copied r_ready r_copied qkv_ready qkv_copied waits").split()))
        block = ctx.enter_context(nc.Block())

        def tiles(eng, body):
            with eng.Fori(0, NT // 2 - 1) as i:
                for r in range(2):
                    body(i * 2 + r, r, True)
            body(NT - 2, 0, True)
            body(NT - 1, 1, False)

        def tile_of(x, n):
            return x[:, bass.ds(n, 1), :].rearrange("p a d -> p (a d)")

        @block.sync
        def _(sp):
            prime(sp, xn_stored)
            sp.dma_start(ident[:, :], t["ident"]).then_inc(w_in, 16)
            for w, name in ((w_o, "woT"), (w_r, "routerT"), (w_qkv, "w_qkv1T")):
                sp.dma_start(w[:, :, :], t[name].rearrange("(k p) i -> p k i", p=P)).then_inc(w_in, 16)

            def store(n, r, more):
                sp.wait_ge(xn_ready, n + 1)
                sp.dma_start(t["xn1"][bass.ds(n, 1)].rearrange("a p d -> p (a d)"), xn[:, r, :])\
                  .then_inc(xn_stored, 16)

            tiles(sp, store)
            sp.wait_ge(xn_stored, 1 + NT * 16)

        @block.gpsimd
        def _(pool):
            def copy(n, r, more):
                pool.wait_ge(yT_ready, 1 + (n + (r - 1) if r else n))
                nc.gpsimd.tensor_copy(y_cur[:, r, :], tile_of(yn, n)).then_inc(y_ready, 1)

            tiles(pool, copy)

        @block.scalar
        def _(act):
            prime(act, yT_copied, xT_copied, r_copied, qkv_copied)
            def copy_yT(n, r):
                act.wait_ge(yT_ready, 1 + n + 1)
                nc.scalar.activation(yT[:, r], ps_yT[:, 0:D].rearrange("p (k c) -> p k c", k=KD),
                                     ACT.Copy).then_inc(yT_copied, 1)

            def root(n):
                act.wait_ge(var_ready, 1 + n + 1)
                nc.scalar.activation(std[:, :], var[:, :], ACT.Sqrt).then_inc(std_ready, 1)

            copy_yT(0, 0)
            root(0)

            def tile(n, r, more):
                if more:
                    copy_yT(n + 1, 1 - r)
                act.wait_ge(xT_ready, 1 + n + 1)
                nc.scalar.activation(xT[:, r], ps_xT[:, 0:D].rearrange("p (k c) -> p k c", k=KD),
                                     ACT.Copy).then_inc(xT_copied, 1)
                if more:
                    root(n + 1)
                act.wait_ge(r_ready, n + 1)
                nc.scalar.activation(tile_of(logits, n), ps_r[:, 0:NE], ACT.Copy).then_inc(r_copied, 1)
                act.wait_ge(qkv_ready, n + 1)
                nc.scalar.activation(tile_of(qkv1, n).rearrange("p (a c) -> p a c", a=2),
                                     ps_qkv[:, r, :, 0:384], ACT.Copy).then_inc(qkv_copied, 1)

            tiles(act, tile)

        @block.vector
        def _(dve):
            prime(dve, var_ready)
            ch = Chain(dve, step)

            def tile(n, r):
                dve.wait_ge(o_ready, n + 1)
                x = tile_of(x_sb, n)
                ch.step(nc.vector.tensor_tensor(x, x, ps_o[:, 0:D], ALU.add))
                apart(dve, waits)
                ch.step(nc.vector.bn_stats(stats[:, :], x))
                apart(dve, waits)
                ch.step(nc.vector.bn_aggr(mv[:, :], stats[:, :]))
                nc.vector.tensor_scalar(var[:, :], mv[:, 1:2], EPS, None, ALU.add).then_inc(var_ready, 1)
                dve.wait_ge(std_ready, n + 1)
                ch.step(nc.vector.reciprocal(rstd[:, :], std[:, :]))
                dve.wait_ge(xT_ready, 1 + (n - 1 if r else n))
                dve.wait_ge(xn_stored, 1 + ((n - 1 if r else n) * 16))
                nc.vector.tensor_scalar(xn[:, r, :], x, mv[:, 0:1], rstd[:, :],
                                        ALU.subtract, ALU.mult).then_inc(xn_ready, 1)

            with dve.Fori(0, NT // 2) as i:
                ch.enter(i, 8)
                for r in range(2):
                    tile(i * 2 + r, r)
                ch.leave(NT // 2, 8)

        @block.tensor
        def _(pe):
            prime(pe, yT_ready, xT_ready)
            pe.wait_ge(w_in, 64)

            def output(n, r):
                pe.wait_ge(y_ready, n + 1)
                pe.wait_ge(yT_copied, 1 + n)
                for k in range(KD):
                    ins = nc.tensor.transpose(ps_yT[:, k * P:(k + 1) * P],
                                              y_cur[:, r, k * P:(k + 1) * P], ident[:, :])
                ins.then_inc(yT_ready, 1)
                pe.wait_ge(yT_copied, 1 + n + 1)
                pe.wait_ge(var_ready, 1 + n)
                for k in range(KD):
                    ins = nc.tensor.matmul(ps_o[:, 0:D], yT[:, r, k, :], w_o[:, k, :],
                                           start=(k == 0), stop=(k == KD - 1))
                ins.then_inc(o_ready, 1)

            output(0, 0)

            def tile(n, r, more):
                if more:
                    output(n + 1, 1 - r)
                pe.wait_ge(xn_ready, n + 1)
                pe.wait_ge(xT_copied, 1 + n)
                for k in range(KD):
                    ins = nc.tensor.transpose(ps_xT[:, k * P:(k + 1) * P],
                                              xn[:, r, k * P:(k + 1) * P], ident[:, :])
                ins.then_inc(xT_ready, 1)
                pe.wait_ge(xT_copied, 1 + n + 1)
                pe.wait_ge(r_copied, 1 + n)
                for k in range(KD):
                    ins = nc.tensor.matmul(ps_r[:, 0:NE], xT[:, r, k, :], w_r[:, k, :],
                                           start=(k == 0), stop=(k == KD - 1))
                ins.then_inc(r_ready, 1)
                pe.wait_ge(qkv_copied, 1 + (n - 1 if r else n))
                for c in range(2):
                    for k in range(KD):
                        ins = nc.tensor.matmul(ps_qkv[:, r, c, 0:384], xT[:, r, k, :],
                                               w_qkv[:, k, c * 384:(c + 1) * 384],
                                               start=(k == 0), stop=(k == KD - 1))
                ins.then_inc(qkv_ready, 1)

            tiles(pe, tile)


def layer1_routing(nc, t, x_sb, qkv1, logits, blocks, inv, v8, val, w):
    ctx = ExitStack()
    with ctx:
        ident = sbuf(ctx, nc, "d_ident", [P, P])
        sums = sbuf(ctx, nc, "d_sums", [P, 2, P], BF16)
        order = sbuf(ctx, nc, "d_order", [P, 2, NG, NG])
        bias = sbuf(ctx, nc, "d_bias", [P, NE])
        tok_id = sbuf(ctx, nc, "d_tok_id", [P, NT])
        iota = sbuf(ctx, nc, "d_iota", [P, NBLK], FP16)
        blk_id = sbuf(ctx, nc, "d_blk_id", [P, 2])
        w_o = sbuf(ctx, nc, "d_w_o", [P, KD, D])
        sc = sbuf(ctx, nc, "d_sc", [P, NT, NE])
        s4 = sbuf(ctx, nc, "d_s4", [P, NT, NE])
        ta = sbuf(ctx, nc, "d_ta", [P, NT * NE])
        tb = sbuf(ctx, nc, "d_tb", [P, NT * NE])
        hi = sbuf(ctx, nc, "d_hi", [P, NT * NG, 4])
        lo = sbuf(ctx, nc, "d_lo", [P, NT * NG, 4])
        hi2 = sbuf(ctx, nc, "d_hi2", [P, NT * NG, 2])
        lo2 = sbuf(ctx, nc, "d_lo2", [P, NT * NG, 2])
        gs = sbuf(ctx, nc, "d_gs", [P, NT, NG])
        gm = sbuf(ctx, nc, "d_gm", [P, NT, NG])
        m8 = sbuf(ctx, nc, "d_m8", [P, NT, 8])
        sel = sbuf(ctx, nc, "d_sel", [P, NT, NE])
        selb = sbuf(ctx, nc, "d_selb", [P, NT, NE], BF16)
        wsum = sbuf(ctx, nc, "d_wsum", [P, NT])
        nb = sbuf(ctx, nc, "d_nb", [P, 3, NE])
        slot_i = sbuf(ctx, nc, "d_slot_i", [P, NT * 8], I32)
        pos_i = sbuf(ctx, nc, "d_pos_i", [P, 2, NT * 8], I32)
        pos = sbuf(ctx, nc, "d_pos", [P, 2, NT * 8])
        be = sbuf(ctx, nc, "d_be", [P, 2])
        be_i = sbuf(ctx, nc, "d_be_i", [P, 2], I32)
        oh_p = sbuf(ctx, nc, "d_oh_p", [P, 4, P], FP16)
        oh_b = sbuf(ctx, nc, "d_oh_b", [P, 4, NBLK], FP16)
        PAIRS = B * (B + 1) // 2
        prod = sbuf(ctx, nc, "d_prod", [P, PAIRS, D])
        prod2 = sbuf(ctx, nc, "d_prod2", [P, PAIRS, D])
        s1 = sbuf(ctx, nc, "d_s1", [P, PAIRS, H1])
        e1 = sbuf(ctx, nc, "d_e1", [P, PAIRS, H1])
        mx = sbuf(ctx, nc, "d_mx", [P, B, H1])
        y1 = sbuf(ctx, nc, "d_y1", [P, 2, D])
        yT = sbuf(ctx, nc, "d_yT", [P, KD, P])

        ps_cum = psum(ctx, nc, "d_ps_cum", [P, 2, 512])
        ps_tot = psum(ctx, nc, "d_ps_tot", [P, 512])
        ps_inv = psum(ctx, nc, "d_ps_inv", [P, 512])
        ps_yT = psum(ctx, nc, "d_ps_yT", [P, 512])
        ps_o = psum(ctx, nc, "d_ps_o", [P, 512])

        (const_in, w_in, step, sig_done, sel_ready, cum_ready, oh_ready, oh_used, be_ready, be_out,
         be_in, qk_ready, qk_used, s_ready, e_ready, p_ready, pv_ready, y_ready, yT_ready,
         yT_copied, o_ready, o_added) = sems(
            ctx, nc, *("d_" + s for s in (
                "const_in w_in step sig_done sel_ready cum_ready oh_ready oh_used be_ready be_out "
                "be_in qk_ready qk_used s_ready e_ready p_ready pv_ready y_ready yT_ready "
                "yT_copied o_ready o_added").split()))
        block = ctx.enter_context(nc.Block())
        pair0 = [l * (l + 1) // 2 for l in range(B)]

        @block.sync
        def _(sp):
            sp.dma_start(sums[:, :, :], t["sums"]).then_inc(const_in, 16)
            sp.dma_start(order[:, :, :, :].rearrange("p a g h -> p (a g h)"),
                         t["order"].partition_broadcast(P)).then_inc(const_in, 16)
            sp.dma_start(bias[:, :], t["router_bias"].partition_broadcast(P)).then_inc(const_in, 16)
            sp.dma_start(tok_id[:, :], t["tok_id"]).then_inc(const_in, 16)
            sp.dma_start(iota[:, :], t["iota"].partition_broadcast(P)).then_inc(const_in, 16)
            sp.dma_start(blk_id[:, :], t["blk_id"]).then_inc(const_in, 16)
            sp.dma_start(ident[:, :], t["ident"]).then_inc(w_in, 16)
            sp.dma_start(w_o[:, :, :], t["wo1T"].rearrange("(k p) i -> p k i", p=P)).then_inc(w_in, 16)
            sp.wait_ge(be_ready, 1)
            sp.dma_start(t["blocks"].rearrange("(c p) -> p c", p=P), be_i[:, :],
                         allow_slow_non_contiguous=True).then_inc(be_out, 16)
            sp.wait_ge(be_out, 16)
            sp.dma_start(blocks[:, :], t["blocks"].rearrange("(a c) -> a c", a=1)).then_inc(be_in, 16)
            sp.wait_ge(be_in, 16)

        @block.gpsimd
        def _(pool):
            for n in range(TPB):
                if n:
                    pool.wait_ge(qk_used, n)
                for l in range(B):
                    q = qkv1[:, l * TPB + n:l * TPB + n + 1, 0:D].to_broadcast([P, l + 1, D])
                    k = qkv1[:, n:n + l * TPB + 1:TPB, D:2 * D]
                    ins = nc.gpsimd.tensor_tensor(prod[:, pair0[l]:pair0[l] + l + 1, :], q, k, ALU.mult)
                ins.then_inc(qk_ready, 1)
                pool.wait_ge(p_ready, n + 1)
                if n:
                    pool.wait_ge(y_ready, n * B)
                for l in range(B):
                    for m in range(l + 1):
                        v = qkv1[:, m * TPB + n, 2 * D:3 * D].rearrange("p (h d) -> p h d", d=DH1)
                        p = e1[:, pair0[l] + m, :].rearrange("p (h a) -> p h a", a=1)\
                            .to_broadcast([P, H1, DH1])
                        ins = nc.gpsimd.tensor_tensor(
                            prod2[:, pair0[l] + m, :].rearrange("p (h d) -> p h d", d=DH1), v, p, ALU.mult)
                ins.then_inc(pv_ready, 1)

        @block.scalar
        def _(act):
            nc.scalar.activation(sc[:, :, :], logits[:, :, :], ACT.Sigmoid).then_inc(sig_done, 1)
            for n in range(TPB):
                act.wait_ge(s_ready, n + 1)
                nc.scalar.activation(e1[:, :, :], s1[:, :, :], ACT.Exp, scale=SCALE1).then_inc(e_ready, 1)
                for l in range(B):
                    i = n * B + l
                    act.wait_ge(yT_ready, i + 1)
                    nc.scalar.activation(yT[:, :, :], ps_yT[:, 0:D].rearrange("p (k c) -> p k c", k=KD),
                                         ACT.Copy).then_inc(yT_copied, 1)

        @block.vector
        def _(dve):
            ch = Chain(dve, step)
            V = nc.vector

            def tt(out, a, b, op):
                ch.step(V.tensor_tensor(out, a, b, op))

            dve.wait_ge(const_in, 96)
            dve.wait_ge(sig_done, 1)
            bc = bias[:, :].rearrange("p (a e) -> p a e", a=1).to_broadcast([P, NT, NE])
            tt(s4[:, :, :], sc[:, :, :], bc, ALU.add)
            v = s4[:, :, :].rearrange("p n (g c) -> p (n g) c", c=EPG)
            tt(hi[:, :, :], v[:, :, 0:4], v[:, :, 4:8], ALU.max)
            tt(lo[:, :, :], v[:, :, 0:4], v[:, :, 4:8], ALU.min)
            tt(hi2[:, :, :], hi[:, :, 0:2], hi[:, :, 2:4], ALU.max)
            tt(hi[:, :, 0:2], hi[:, :, 0:2], hi[:, :, 2:4], ALU.min)
            tt(lo[:, :, 0:2], lo[:, :, 0:2], lo[:, :, 2:4], ALU.max)
            tt(lo2[:, :, :], hi[:, :, 0:2], lo[:, :, 0:2], ALU.max)
            tt(hi[:, :, 0], hi2[:, :, 0], hi2[:, :, 1], ALU.max)
            tt(hi[:, :, 1], hi2[:, :, 0], hi2[:, :, 1], ALU.min)
            tt(lo[:, :, 0], lo2[:, :, 0], lo2[:, :, 1], ALU.max)
            tt(lo[:, :, 1], hi[:, :, 1], lo[:, :, 0], ALU.max)
            tt(gs[:, :, :].rearrange("p n g -> p (n g)"), hi[:, :, 0], lo[:, :, 1], ALU.add)
            gg = [P, NT * NG, NG]
            mine = gs[:, :, :].rearrange("p n (g a) -> p (n g) a", a=1).to_broadcast(gg)
            for i in range(NT):
                sl = slice(i * NG, (i + 1) * NG)
                others = gs[:, i:i + 1, :].to_broadcast([P, NG, NG])
                a = ta[:, :].rearrange("p (x h) -> p x h", h=NG)[:, sl]
                b = tb[:, :].rearrange("p (x h) -> p x h", h=NG)[:, sl]
                ch.did(V.tensor_tensor(a, others, mine[:, sl], ALU.is_ge))
                ch.did(V.tensor_tensor(b, others, mine[:, sl], ALU.is_gt))
            ch.last()
            for x, y in ((ta, 0), (tb, 1)):
                x4 = x[:, :].rearrange("p (n g) -> p n g", g=NG * NG)
                o = order[:, y:y + 1].rearrange("p a g h -> p a (g h)").to_broadcast([P, NT, NG * NG])
                tt(x4, x4, o, ALU.mult)
            tt(ta[:, :], ta[:, :], tb[:, :], ALU.add)
            ch.step(V.tensor_reduce(gm[:, :, :].rearrange("p n g -> p (n g)"),
                                    ta[:, :].rearrange("p (x h) -> p x h", h=NG), AX.X, ALU.add))
            ch.step(V.tensor_scalar(gm[:, :, :], gm[:, :, :], float(TOPG), None, ALU.is_lt))
            tmp = ta[:, :].rearrange("p (n e) -> p n e", e=NE)
            tt(ta[:, :].rearrange("p (x c) -> p x c", c=EPG), v,
               gm[:, :, :].rearrange("p n (g a) -> p (n g) a", a=1).to_broadcast([P, NT * NG, EPG]),
               ALU.mult)
            ch.step(V.tensor_scalar(ta[:, :], ta[:, :], 0.0, None, ALU.add))
            rep = tb[:, :].rearrange("p (n e) -> p n e", e=NE)
            for i in range(NT):
                ch.did(V.max(m8[:, i, :], tmp[:, i, :]))
            ch.last()
            for i in range(NT):
                ch.did(V.match_replace(rep[:, i, :], m8[:, i, :], tmp[:, i, :], -3e38))
            ch.last()
            tt(sel[:, :, :], tmp, rep, ALU.not_equal)
            V.tensor_copy(selb[:, :, :], sel[:, :, :]).then_inc(sel_ready, 1)
            tt(w[:, :, :], sc[:, :, :], sel[:, :, :], ALU.mult)
            ch.step(V.tensor_reduce(wsum[:, :], w[:, :, :], AX.X, ALU.add))
            ch.step(V.tensor_scalar(wsum[:, :], wsum[:, :], 1e-20, None, ALU.add))
            ch.step(V.reciprocal(wsum[:, :], wsum[:, :]))
            ch.step(V.tensor_scalar(wsum[:, :], wsum[:, :], RSCALE, None, ALU.mult))
            tt(w[:, :, :], w[:, :, :],
               wsum[:, :].rearrange("p (n a) -> p n a", a=1).to_broadcast([P, NT, NE]), ALU.mult)
            dve.wait_ge(cum_ready, 1)
            ch.step(V.tensor_scalar(nb[:, 0, :], ps_tot[:, 0:NE], (P - 1) / 2, 1.0 / P, ALU.add, ALU.mult))
            ch.step(V.tensor_scalar(nb[:, 0, :], nb[:, 0, :], 2.0 ** 23, None, ALU.add))
            ch.step(V.tensor_scalar(nb[:, 0, :], nb[:, 0, :], -2.0 ** 23, None, ALU.add))
            src = 0
            for k in range(6):
                a, b = nb[:, src, :], nb[:, 1 + k % 2, :]
                ch.did(V.tensor_copy(b[:, 0:1 << k], a[:, 0:1 << k]))
                tt(b[:, 1 << k:NE], a[:, 1 << k:NE], a[:, 0:NE - (1 << k)], ALU.add)
                src = 1 + k % 2
            incl, base = nb[:, src, :], nb[:, 3 - src, :]
            for c in range(2):
                tt(ta[:, c * NE:(c + 1) * NE], incl, blk_id[:, c:c + 1].to_broadcast([P, NE]), ALU.is_le)
            ch.step(V.tensor_reduce(be[:, :], ta[:, 0:2 * NE].rearrange("p (c e) -> p c e", c=2),
                                    AX.X, ALU.add))
            ch.step(V.tensor_scalar(be[:, :], be[:, :], NE - 1.0, None, ALU.min))
            V.tensor_copy(be_i[:, :], be[:, :]).then_inc(be_ready, 1)
            tt(base, incl, nb[:, 0, :], ALU.subtract)
            ch.step(V.tensor_scalar(base, base, float(P), 1.0, ALU.mult, ALU.add))
            tt(val[:, :, :], ps_cum[:, :, :].rearrange("p a (n e) -> p (a n) e", e=NE),
               base.rearrange("p (a e) -> p a e", a=1).to_broadcast([P, NT, NE]), ALU.add)
            tt(val[:, :, :], val[:, :, :], sel[:, :, :], ALU.mult)
            for i in range(NT):
                ch.did(V.max(v8[:, i, :], val[:, i, :]))
            ch.last()
            ch.step(V.tensor_scalar(slot_i[:, :], v8[:, :, :].rearrange("p n k -> p (n k)"),
                                    -1.0, None, ALU.add))
            ch.did(V.tensor_scalar(pos_i[:, 0, :], slot_i[:, :], P - 1, None, ALU.bitwise_and))
            ch.step(V.tensor_scalar(pos_i[:, 1, :], slot_i[:, :], 7, None, ALU.logical_shift_right))
            ch.step(V.tensor_copy(pos[:, :, :], pos_i[:, :, :]))
            for j in range(NT * 8):
                if j >= 4:
                    dve.wait_ge(oh_used, j - 3)
                V.tensor_scalar(oh_p[:, j % 4, :], iota[:, 0:P], pos[:, 0, j:j + 1],
                                tok_id[:, j // 8:j // 8 + 1], ALU.is_equal, ALU.mult).then_inc(oh_ready, 1)
                V.tensor_scalar(oh_b[:, j % 4, :], iota[:, :], pos[:, 1, j:j + 1], None,
                                ALU.is_equal).then_inc(oh_ready, 1)
            dve.wait_ge(oh_used, NT * 8)
            ch.step(V.tensor_copy(inv[:, :], ps_inv[:, 0:NBLK]))

            def add(n, l):
                i = n * B + l
                dve.wait_ge(o_ready, i + 1)
                V.tensor_tensor(x_sb[:, l * TPB + n, :], x_sb[:, l * TPB + n, :], ps_o[:, 0:D],
                                ALU.add).then_inc(o_added, 1)

            for n in range(TPB):
                dve.wait_ge(qk_ready, n + 1)
                if n:
                    dve.wait_ge(e_ready, n)
                V.tensor_reduce(s1[:, :, :].rearrange("p a h -> p (a h)"),
                                prod[:, :, :].rearrange("p a (h d) -> p (a h) d", d=DH1),
                                AX.X, ALU.add).then_inc(qk_used, 1)
                dve.wait_ge(qk_used, n + 1)
                for l in range(B):
                    a = s1[:, pair0[l]:pair0[l] + l + 1, :]
                    ch.did(V.tensor_reduce(mx[:, l, :], a.rearrange("p m h -> p h m"), AX.X, ALU.max))
                ch.last()
                for l in range(B):
                    a = s1[:, pair0[l]:pair0[l] + l + 1, :]
                    ins = V.tensor_tensor(a, a, mx[:, l:l + 1, :].to_broadcast([P, l + 1, H1]),
                                          ALU.subtract)
                ins.then_inc(s_ready, 1)
                dve.wait_ge(e_ready, n + 1)
                for l in range(B):
                    a = e1[:, pair0[l]:pair0[l] + l + 1, :]
                    ch.did(V.tensor_reduce(mx[:, l, :], a.rearrange("p m h -> p h m"), AX.X, ALU.add))
                ch.last()
                ch.step(V.reciprocal(mx[:, :, :], mx[:, :, :]))
                for l in range(B):
                    a = e1[:, pair0[l]:pair0[l] + l + 1, :]
                    ins = V.tensor_tensor(a, a, mx[:, l:l + 1, :].to_broadcast([P, l + 1, H1]), ALU.mult)
                ins.then_inc(p_ready, 1)
                dve.wait_ge(pv_ready, n + 1)
                for l in range(B):
                    i = n * B + l
                    if i >= 2:
                        dve.wait_ge(yT_ready, i - 1)
                    ins = V.tensor_reduce(y1[:, i % 2, :],
                                          prod2[:, pair0[l]:pair0[l] + l + 1, :]
                                          .rearrange("p m d -> p d m"), AX.X, ALU.add)
                    ins.then_inc(y_ready, 1)
                    if l:
                        add(n, l - 1)
                add(n, B - 1)

        @block.tensor
        def _(pe):
            pe.wait_ge(const_in, 96)
            pe.wait_ge(sel_ready, 1)
            half = NT // 2
            for a in range(2):
                nc.tensor.matmul(ps_cum[:, a, :], sums[:, 0, :],
                                 selb[:, a * half:(a + 1) * half, :].rearrange("p n e -> p (n e)"),
                                 start=True, stop=False, skip_group_check=True)
                last = (a + 1) * half - 1
                for i in range(last):
                    first = max(a * half, i + 1)
                    n = last + 1 - first
                    nc.tensor.matmul(ps_cum[:, a, (first - a * half) * NE:512].rearrange(
                                         "p (n e) -> p n e", e=NE),
                                     sums[:, 1, :], selb[:, i:i + 1, :].to_broadcast([P, n, NE]),
                                     start=False, stop=(i == last - 1), skip_group_check=True)
            for i in range(NT):
                ins = nc.tensor.matmul(ps_tot[:, 0:NE], sums[:, 1, :], selb[:, i, :],
                                       start=(i == 0), stop=(i == NT - 1))
            ins.then_inc(cum_ready, 1)
            for j in range(NT * 8):
                pe.wait_ge(oh_ready, 2 * (j + 1))
                nc.tensor.matmul(ps_inv[:, 0:NBLK], oh_p[:, j % 4, :], oh_b[:, j % 4, :],
                                 start=(j == 0), stop=(j == NT * 8 - 1)).then_inc(oh_used, 1)
            pe.wait_ge(w_in, 32)
            for i in range(NT):
                pe.wait_ge(y_ready, i + 1)
                pe.wait_ge(yT_copied, i)
                for k in range(KD):
                    ins = nc.tensor.transpose(ps_yT[:, k * P:(k + 1) * P],
                                              y1[:, i % 2, k * P:(k + 1) * P], ident[:, :])
                ins.then_inc(yT_ready, 1)
                pe.wait_ge(yT_copied, i + 1)
                pe.wait_ge(o_added, i)
                for k in range(KD):
                    ins = nc.tensor.matmul(ps_o[:, 0:D], yT[:, k, :], w_o[:, k, :],
                                           start=(k == 0), stop=(k == KD - 1))
                ins.then_inc(o_ready, 1)


def layer1_experts(nc, t, block_expert, inv):
    ctx = ExitStack()
    with ctx:
        NS = 4
        ident = sbuf(ctx, nc, "e_ident", [P, P])
        w_gu = sbuf(ctx, nc, "e_w_gu", [P, NS, 2, KD, INTER1])
        w_d = sbuf(ctx, nc, "e_w_d", [HI1, NS, 2, D])
        idx = sbuf(ctx, nc, "e_idx", [P, NS], U32)
        x = sbuf(ctx, nc, "e_x", [P, NS, D])
        xT = sbuf(ctx, nc, "e_xT", [P, KD, P])
        sg = sbuf(ctx, nc, "e_sg", [P, INTER1])
        h = sbuf(ctx, nc, "e_h", [P, INTER1])
        hT = sbuf(ctx, nc, "e_hT", [HI1, 2, P])
        y = sbuf(ctx, nc, "e_y", [P, NS, D])

        ps_xT = psum(ctx, nc, "e_ps_xT", [P, 512])
        ps_gu = psum(ctx, nc, "e_ps_gu", [P, 2, 512])
        ps_hT = psum(ctx, nc, "e_ps_hT", [P, 512])
        ps_y = psum(ctx, nc, "e_ps_y", [P, 512])

        (const_in, idx_ready, xT_ready, xT_copied, gu_ready, silu_ready, h_ready, hT_ready,
         hT_copied, y_ready, y_copied, waits) = sems(
            ctx, nc, *("e_" + s for s in (
                "const_in idx_ready xT_ready xT_copied gu_ready silu_ready h_ready hT_ready "
                "hT_copied y_ready y_copied waits").split()))
        gu_in, d_in, x_in, y_out = (sems(ctx, nc, *(f"e_{s}{i}" for i in range(NS)))
                                    for s in ("gu_in", "d_in", "x_in", "y_out"))
        block = ctx.enter_context(nc.Block())

        def all_blocks(eng, body):
            for j in range(NS):
                body(j, j, False)
            with eng.Fori(1, NBLK // NS) as i:
                for c in range(NS):
                    body(i * NS + c, c, True)

        def steps(eng, body):
            with eng.Fori(0, NBLK // NS - 1) as i:
                for c in range(1, NS + 1):
                    body(i * NS + c, i, c, True)
            for c in range(1, NS):
                body(NBLK - NS + c, NBLK // NS - 1, c, c < NS - 1)

        def slot(i, c):
            return c % NS, i + 1 + c // NS

        @block.sync
        def _(sp):
            sp.dma_start(ident[:, :], t["ident"]).then_inc(const_in, 16)

            def load(j, s, free):
                e = sp.value_load(block_expert[0:1, bass.ds(j, 1)], min_val=0, max_val=NE - 1)
                if free:
                    sp.wait_ge(gu_ready, j - (NS - 1))
                for m, name in enumerate(("e_gate", "e_up")):
                    sp.dma_start(w_gu[:, s, m],
                                 t[name][bass.ds(e, 1)].rearrange("a p k i -> p (a k) i"))\
                      .then_inc(gu_in[s], 16)
                if free:
                    sp.wait_ge(y_ready, 1 + j - (NS - 1))
                sp.dma_start(w_d[:, s],
                             t["e_down"][bass.ds(e, 1)].rearrange("a p k d -> p (a k) d"))\
                  .then_inc(d_in[s], 16)

            all_blocks(sp, load)

        @block.gpsimd
        def _(pool):
            def gather(j, s, free):
                if free:
                    pool.wait_ge(xT_ready, j - (NS - 1))
                nc.gpsimd.tensor_copy(idx[:, s:s + 1], inv[:, bass.ds(j, 1)]).then_inc(idx_ready, 1)
                pool.wait_ge(idx_ready, j + 1)
                apart(pool, waits)
                pool.indirect_dma_start(x[:, s, :], None, t["xn1"].rearrange("n p d -> (n p) d"),
                                        bass.IndirectOffsetOnAxis(idx[:, s:s + 1], 0))\
                    .then_inc(x_in[s], 16)

            all_blocks(pool, gather)

        @block.scalar
        def _(act):
            prime(act, y_copied, *y_out)
            def silu(j, c):
                act.wait_ge(gu_ready, j + 1)
                act.wait_ge(h_ready, j)
                nc.scalar.activation(sg[:, :], ps_gu[:, c % 2, 0:INTER1], ACT.Silu)\
                  .then_inc(silu_ready, 1)

            def store(j, i, c):
                s, use = slot(i, c)
                act.wait_ge(y_ready, 1 + j + 1)
                act.wait_ge(y_out[s], 1 + (use - 1) * 16)
                nc.scalar.activation(y[:, s, :], ps_y[:, 0:D], ACT.Copy).then_inc(y_copied, 1)
                act.wait_ge(y_copied, 1 + j + 1)
                act.dma_start(t["slots"][bass.ds(j, 1)].rearrange("a p d -> p (a d)"), y[:, s, :])\
                   .then_inc(y_out[s], 16)

            silu(0, 0)

            def step(j, i, c, more):
                silu(j, c)
                store(j - 1, i, c - 1)

            steps(act, step)
            store(NBLK - 1, NBLK // NS - 1, NS - 1)
            for s in range(NS):
                act.wait_ge(y_out[s], 1 + NBLK // NS * 16)

        @block.vector
        def _(dve):
            prime(dve, hT_copied)
            def copy_x(j):
                dve.wait_ge(xT_ready, j + 1)
                nc.vector.tensor_copy(xT[:, :, :].rearrange("p k c -> p (k c)"), ps_xT[:, 0:D])\
                  .then_inc(xT_copied, 1)

            def gate(j, c):
                dve.wait_ge(silu_ready, j + 1)
                dve.wait_ge(hT_ready, j)
                nc.vector.tensor_tensor(h[:, :], sg[:, :], ps_gu[:, c % 2, INTER1:2 * INTER1],
                                        ALU.mult).then_inc(h_ready, 1)

            def copy_h(j):
                dve.wait_ge(hT_ready, j + 1)
                dve.wait_ge(y_ready, 1 + j)
                nc.vector.tensor_copy(hT[:, :, :].rearrange("p k c -> p (k c)"), ps_hT[0:HI1, 0:2 * P])\
                  .then_inc(hT_copied, 1)

            copy_x(0)
            gate(0, 0)
            copy_x(1)

            def step(j, i, c, more):
                copy_h(j - 1)
                gate(j, c)
                if more:
                    copy_x(j + 1)

            steps(dve, step)
            copy_h(NBLK - 1)

        @block.tensor
        def _(pe):
            prime(pe, y_ready)
            pe.wait_ge(const_in, 16)

            def transpose_x(j, i, c):
                s, use = slot(i, c)
                pe.wait_ge(x_in[s], use * 16)
                pe.wait_ge(xT_copied, j)
                for k in range(KD):
                    ins = nc.tensor.transpose(ps_xT[:, k * P:(k + 1) * P],
                                              x[:, s, k * P:(k + 1) * P], ident[:, :])
                ins.then_inc(xT_ready, 1)

            def gate_up(j, i, c):
                s, use = slot(i, c)
                pe.wait_ge(xT_copied, j + 1)
                pe.wait_ge(gu_in[s], use * 32)
                for k in range(KD):
                    ins = nc.tensor.matmul(
                        ps_gu[:, c % 2, 0:2 * INTER1].rearrange("p (m i) -> p m i", m=2),
                        xT[:, k, :], w_gu[:, s, :, k, :], start=(k == 0), stop=(k == KD - 1))
                ins.then_inc(gu_ready, 1)

            def transpose_h(j):
                pe.wait_ge(h_ready, j + 1)
                pe.wait_ge(hT_copied, 1 + j)
                for k in range(2):
                    ins = nc.tensor.transpose(ps_hT[0:HI1, k * P:(k + 1) * P],
                                              h[:, k * HI1:(k + 1) * HI1], ident[:, :])
                ins.then_inc(hT_ready, 1)

            def down(j, i, c):
                s, use = slot(i, c)
                pe.wait_ge(hT_copied, 1 + j + 1)
                pe.wait_ge(d_in[s], use * 16)
                pe.wait_ge(y_copied, 1 + j)
                for k in range(2):
                    ins = nc.tensor.matmul(ps_y[:, 0:D], hT[:, k, :], w_d[:, s, k, :],
                                           start=(k == 0), stop=(k == 1))
                ins.then_inc(y_ready, 1)

            transpose_x(0, 0, 0)
            gate_up(0, 0, 0)
            transpose_x(1, 0, 1)

            def step(j, i, c, more):
                transpose_h(j - 1)
                gate_up(j, i, c)
                if more:
                    transpose_x(j + 1, i, c + 1)
                down(j - 1, i, c - 1)

            steps(pe, step)
            transpose_h(NBLK - 1)
            down(NBLK - 1, NBLK // NS - 1, NS - 1)


def layer1_combine(nc, t, x_sb, v8, val, w):
    ctx = ExitStack()
    with ctx:
        slots = sbuf(ctx, nc, "f_slots", [P, NT * TOPK], U32)
        idx = sbuf(ctx, nc, "f_idx", [P, 2, TOPK], U32)
        rows = sbuf(ctx, nc, "f_rows", [P, 2, TOPK, D])
        eq = sbuf(ctx, nc, "f_eq", [P, TOPK, NE])
        w8 = sbuf(ctx, nc, "f_w8", [P, TOPK])
        slots_ready, idx_ready, step, summed, stored, waits = sems(
            ctx, nc, "f_slots_ready", "f_idx_ready", "f_step", "f_summed", "f_stored", "f_waits")
        rows_in = [sems(ctx, nc, *(f"f_rows_in{r}_{k}" for k in range(TOPK))) for r in range(2)]
        block = ctx.enter_context(nc.Block())

        @block.sync
        def _(sp):
            with sp.Fori(0, NT) as n:
                sp.wait_ge(summed, 1 + n + 1)
                sp.dma_start(t["out"].rearrange("(n p) d -> n p d", p=P)[bass.ds(n, 1)]
                             .rearrange("a p d -> p (a d)"),
                             x_sb[:, bass.ds(n, 1), :].rearrange("p a d -> p (a d)"))\
                  .then_inc(stored, 16)
            sp.wait_ge(stored, NT * 16)

        @block.gpsimd
        def _(pool):
            pool.wait_ge(slots_ready, 1)
            with pool.Fori(0, NT // 2) as i:
                for r in range(2):
                    n = i * 2 + r
                    pool.wait_ge(summed, 1 + (n - 1 if r else n))
                    nc.gpsimd.tensor_copy(idx[:, r, :], slots[:, bass.ds(n * TOPK, TOPK)])\
                      .then_inc(idx_ready, 1)
                    pool.wait_ge(idx_ready, n + 1)
                    apart(pool, waits)
                    for k in range(TOPK):
                        pool.indirect_dma_start(rows[:, r, k, :], None,
                                                t["slots"].rearrange("n p d -> (n p) d"),
                                                bass.IndirectOffsetOnAxis(idx[:, r, k:k + 1], 0))\
                            .then_inc(rows_in[r][k], 16)

        @block.vector
        def _(dve):
            prime(dve, summed)
            V = nc.vector
            ch = Chain(dve, step)
            V.tensor_scalar(slots[:, :], v8[:, :, :].rearrange("p n k -> p (n k)"), -1.0, None,
                            ALU.add).then_inc(slots_ready, 1)
            PER = 2 * (3 + TOPK - 1)
            with dve.Fori(0, NT // 2) as i:
                ch.enter(i, PER)
                for r in range(2):
                    n = i * 2 + r
                    v = val[:, bass.ds(n, 1), :].to_broadcast([P, TOPK, NE])
                    v_k = v8[:, bass.ds(n, 1), :].rearrange("p a k -> p k a").to_broadcast([P, TOPK, NE])
                    ch.step(V.tensor_tensor(eq[:, :, :], v, v_k, ALU.is_equal))
                    ch.step(V.tensor_tensor(eq[:, :, :], eq[:, :, :],
                                            w[:, bass.ds(n, 1), :].to_broadcast([P, TOPK, NE]), ALU.mult))
                    ch.step(V.tensor_reduce(w8[:, :], eq[:, :, :], AX.X, ALU.add))
                    x = x_sb[:, bass.ds(n, 1), :].rearrange("p a d -> p (a d)")
                    for k in range(TOPK):
                        dve.wait_ge(rows_in[r][k], (i + 1) * 16)
                        ins = V.scalar_tensor_tensor(x, rows[:, r, k, :], w8[:, k:k + 1], x,
                                                     ALU.mult, ALU.add)
                        if k < TOPK - 1:
                            ch.step(ins)
                        else:
                            ins.then_inc(summed, 1)
                ch.leave(NT // 2, PER)


def kernel_program(nc, t):
    ctx = ExitStack()
    with ctx:
        x_sb = sbuf(ctx, nc, "x_sb", [P, NT, D])
        yn = sbuf(ctx, nc, "yn", [P, NT, D])
        with nc.sbuf_tensor("v_pad", [P, NT, HKV, VW], F32) as v_pad:
            layer0_dense(nc, t, x_sb, v_pad)
            layer0_attention(nc, t, v_pad, yn)
        v8 = sbuf(ctx, nc, "v8", [P, NT, 8])
        val = sbuf(ctx, nc, "val", [P, NT, NE])
        w = sbuf(ctx, nc, "w_full", [P, NT, NE])
        inv = sbuf(ctx, nc, "inv", [P, NBLK], U32)
        blocks = sbuf(ctx, nc, "block_expert", [1, 2 * P], I32)
        with nc.sbuf_tensor("qkv1", [P, NT, 3 * D], F32) as qkv1, \
                nc.sbuf_tensor("logits", [P, NT, NE], F32) as logits:
            layer1_front(nc, t, x_sb, yn, qkv1, logits)
            layer1_routing(nc, t, x_sb, qkv1, logits, blocks, inv, v8, val, w)
        layer1_experts(nc, t, blocks, inv)
        layer1_combine(nc, t, x_sb, v8, val, w)


def constants():
    c = {}
    h = np.array([[1.0]])
    while h.shape[0] < P:
        h = np.block([[h, h], [h, -h]])
    c["had"] = np.stack([h / 16, -h / 16, h / 32], axis=1).astype(np.float32)
    c["ident"] = np.eye(P, dtype=np.float32)
    causal = np.where(np.arange(P)[None, :] > np.arange(P)[:, None], -3e38, 0.0)
    c["causal"] = np.stack([causal, causal.T], axis=1).astype(np.dtype("bfloat16"))
    before = np.arange(P)[:, None] < np.arange(P)[None, :]
    c["sums"] = np.stack([before, np.ones((P, P))], axis=1).astype(np.dtype("bfloat16"))
    g = np.arange(NG)
    c["order"] = np.stack([g[None, :] < g[:, None], g[None, :] > g[:, None]])\
        .astype(np.float32).reshape(-1)
    c["tok_id"] = (np.arange(P)[:, None] + P * np.arange(NT)[None, :]).astype(np.float32)
    c["blk_id"] = (np.arange(P)[:, None] + P * np.arange(2)[None, :]).astype(np.float32)
    c["iota"] = np.arange(NBLK).astype(np.float16)
    pad = np.zeros((2, SROWS - MROW, T))
    pad[1, 0:NP_] = 1.0
    c["pad"] = pad.astype(np.dtype("bfloat16"))
    c["identb"] = np.eye(P).astype(np.dtype("bfloat16"))
    theta = (1.0 / 10000.0 ** (np.arange(0, HD, 2, dtype=np.float32) / HD)).astype(np.float32)
    freqs = np.arange(T, dtype=np.float32)[:, None] * theta[None, :]
    cos = np.repeat(np.cos(freqs), 2, axis=1)
    sin = np.stack([-np.sin(freqs), np.sin(freqs)], axis=-1).reshape(T, HD)
    c["rope"] = np.stack([cos, sin], axis=1).astype(np.float32).reshape(TPB, P, 2, HD)\
        .transpose(1, 0, 2, 3)
    return c


def kernel(**inputs):
    import numpy as _np
    import concourse.bacc as _bacc
    from concourse import mybir as _mybir
    from concourse.bass_utils import run_bass_kernel_spmd as _run

    a = {k: _np.asarray(v) for k, v in inputs.items()}
    given = constants()
    given["x"] = a["L0_attn_x"].reshape(TOK, D)
    for name, key in (("wqT", "L0_attn_wq"), ("wkT", "L0_attn_wk"), ("wvT", "L0_attn_wv"),
                      ("woT", "L0_attn_wo"), ("w_upT", "L0_ffn_W_up"), ("w_gateT", "L0_ffn_W_gate"),
                      ("w_downT", "L0_ffn_W_down"), ("w_qkv1T", "L1_attn_weight_qkv"),
                      ("wo1T", "L1_attn_weight_out"), ("routerT", "L1_ffn_gate_weight")):
        given[name] = a[key].T
    for name, key in (("su_ug", "L0_ffn_SU_ug"), ("su_dp", "L0_ffn_SU_dp"),
                      ("ws_ug", "L0_ffn_Wscale_ug"), ("ws_dp", "L0_ffn_Wscale_dp"),
                      ("router_bias", "L1_ffn_e_score_correction_bias")):
        given[name] = a[key]
    for name, key in (("e_gate", "L1_ffn_gate_proj"), ("e_up", "L1_ffn_up_proj")):
        given[name] = a[key].reshape(NE, INTER1, KD, P).transpose(0, 3, 2, 1)
    given["e_down"] = a["L1_ffn_down_proj"].reshape(NE, D, 2, HI1).transpose(0, 3, 2, 1)

    nc = _bacc.Bacc("TRN2", target_bir_lowering=False, num_devices=1)
    arrays, t = {}, {}
    for name, v in given.items():
        arrays[name] = _np.ascontiguousarray(v)
        t[name] = nc.dram_tensor(name, arrays[name].shape, _mybir.dt.from_np(arrays[name].dtype),
                                 kind="ExternalInput").ap()
    for name, (shape, dt) in SCRATCH.items():
        t[name] = nc.dram_tensor(name, shape, dt).ap()
    t["out"] = nc.dram_tensor("out", (TOK, D), F32, kind="ExternalOutput").ap()
    kernel_program(nc, t)
    r = _run(nc, [arrays], core_ids=[0])
    return r.results[0]["out"].reshape(B, T, D)
```

```python
import numpy as np
from contextlib import ExitStack
import concourse.bass as bass
from concourse import mybir

F32 = mybir.dt.float32
BF16 = mybir.dt.bfloat16
FP16 = mybir.dt.float16
U32 = mybir.dt.uint32
I32 = mybir.dt.int32
ALU = mybir.AluOpType
ACT = mybir.ActivationFunctionType
AX = mybir.AxisListType

P = 128
B, T, D = 4, 512, 256
TOK = B * T
NT = TOK // P
TPB = T // P
KD = D // P
EPS = 1e-5

H0, HKV, HD = 32, 8, 8
REP = H0 // HKV
QK = H0 * HD + HKV * HD
QKV = QK + HKV * HD
SCALE0 = HD ** -0.5
NP_ = 3
NC_ = NP_ * NP_
SROWS = 96
MROW = NC_ * HD
VW = 32

INTER0 = 1024
NI0 = INTER0 // P

H1, DH1 = 16, 16
SCALE1 = DH1 ** -0.5

NE, TOPK, NG, TOPG = 64, 8, 8, 4
EPG = NE // NG
INTER1 = 176
HI1 = INTER1 // 2
RSCALE = 2.5
NBLK = (TOK * TOPK + NE * (P - 1)) // P + 1
BPN = 48
assert NBLK <= TPB * BPN
NBLK = TPB * BPN
NLOAD = NBLK + 4
ROW = D + NE


SCRATCH = {
    "qk_parts": ((B, NP_ * 2 + 2, P, T), BF16),
    "rows": ((TOK + P, ROW), F32),
    "sums_a": ((TOK + P, D), F32),
    "sums_b": ((TOK + P, D), F32),
    "blocks": ((2 * P,), I32),
    "blocks_f": ((2 * P,), F32),
}


def sbuf(ctx, nc, name, shape, dt=F32):
    return ctx.enter_context(nc.sbuf_tensor(name, shape, dt))


def psum(ctx, nc, name, shape, dt=F32):
    return ctx.enter_context(nc.psum_tensor(name, shape, dt))


def sems(ctx, nc, *names):
    return [ctx.enter_context(nc.semaphore(n)) for n in names]


def prime(eng, *semaphores):
    for s in semaphores:
        eng.sem_inc(s, 1)


def apart(eng, sem):
    eng.sem_inc(sem, 1)


class Chain:

    def __init__(self, eng, sem):
        self.eng, self.sem, self.base, self.n = eng, sem, 0, 0

    def did(self, ins):
        ins.then_inc(self.sem, 1)
        self.n += 1

    def last(self):
        self.eng.wait_ge(self.sem, self.base + self.n)

    def step(self, ins):
        self.did(ins)
        self.last()

    def enter(self, i, per):
        self.start = self.n
        self.base = i * per

    def leave(self, count, per):
        assert self.n - self.start == per, (self.n - self.start, per)
        self.base, self.n = 0, self.start + count * per


def layer0_dense(nc, t, x_sb, v_pad):
    ctx = ExitStack()
    with ctx:
        ident = sbuf(ctx, nc, "a_ident", [P, P])
        identb = sbuf(ctx, nc, "a_identb", [P, P], BF16)
        had = sbuf(ctx, nc, "a_had", [P, 3, P])
        w_qkv = sbuf(ctx, nc, "a_w_qkv", [P, KD, QKV])
        rope = sbuf(ctx, nc, "a_rope", [P, TPB, 2, HD])
        w_raw = sbuf(ctx, nc, "a_w_raw", [P, KD, 2, INTER0])
        w_gu = sbuf(ctx, nc, "a_w_gu", [P, KD, 2, INTER0])
        wd_raw = sbuf(ctx, nc, "a_wd_raw", [P, NI0, D])
        wd_a = sbuf(ctx, nc, "a_wd_a", [P, NI0, D])
        wd_b = sbuf(ctx, nc, "a_wd_b", [P, NI0, D])
        w_down = sbuf(ctx, nc, "a_w_down", [P, NI0, D])
        su_ug = sbuf(ctx, nc, "a_su_ug", [P, KD])
        su_dp = sbuf(ctx, nc, "a_su_dp", [P, NI0])
        ws_ug = sbuf(ctx, nc, "a_ws_ug", [P, 2, NI0])
        ws_dp = sbuf(ctx, nc, "a_ws_dp", [P, D])
        stats = sbuf(ctx, nc, "a_stats", [P, TPB, 6])
        mv = sbuf(ctx, nc, "a_mv", [P, TPB, 2])
        var = sbuf(ctx, nc, "a_var", [P, TPB])
        std = sbuf(ctx, nc, "a_std", [P, TPB])
        rstd = sbuf(ctx, nc, "a_rstd", [P, TPB])
        xn = sbuf(ctx, nc, "a_xn", [P, TPB, D])
        xnT = sbuf(ctx, nc, "a_xnT", [P, KD, T])
        qk = sbuf(ctx, nc, "a_qk", [P, TPB, QK])
        rot = sbuf(ctx, nc, "a_rot", [P, QK])
        rot_b = sbuf(ctx, nc, "a_rot_b", [P, QK])
        rest = sbuf(ctx, nc, "a_rest", [P, QK])
        parts_q = sbuf(ctx, nc, "a_parts_q", [P, 2, NP_, H0 * HD], BF16)
        parts_k = sbuf(ctx, nc, "a_parts_k", [P, 2, NP_, HKV * HD], BF16)
        stage = sbuf(ctx, nc, "a_stage", [P, NP_ * 2 + 2, T], BF16)
        sg = sbuf(ctx, nc, "a_sg", [P, 2, T])
        hT = sbuf(ctx, nc, "a_hT", [P, NI0, T])

        ps_gu = psum(ctx, nc, "a_ps_gu", [P, 4, 512])
        ps_x = psum(ctx, nc, "a_ps_x", [P, 2, 512])
        ps_qkv = psum(ctx, nc, "a_ps_qkv", [P, 512])
        ps_parts = psum(ctx, nc, "a_ps_parts", [P, 8, P], BF16)

        (const_in, had_in, wgu_in, wd_in, wqkv_in, scale_in, dve_step, had_ready, had_copied,
         down_had, down_copied, var_ready, std_ready, xn_ready, xT_ready, xT_copied,
         qkv_ready, qkv_copied, parts_ready, partsT_ready, partsT_copied, stored, gu_ready,
         silu_ready, h_ready, down_ready, added, w_ready, v_clear, waits) = sems(
            ctx, nc, *("a_" + s for s in (
                "const_in had_in wgu_in wd_in wqkv_in scale_in dve_step had_ready had_copied "
                "down_had down_copied var_ready std_ready xn_ready xT_ready xT_copied "
                "qkv_ready qkv_copied parts_ready partsT_ready partsT_copied stored gu_ready "
                "silu_ready h_ready down_ready added w_ready v_clear waits").split()))
        x_in = sems(ctx, nc, *(f"a_x_in{b}" for b in range(B)))
        block = ctx.enter_context(nc.Block())

        @block.sync
        def _(sp):
            prime(sp, stored)
            sp.dma_start(had[:, :, :], t["had"]).then_inc(had_in, 16)
            for m, name in enumerate(("w_gateT", "w_upT")):
                sp.dma_start(w_raw[:, :, m, :],
                             t[name].rearrange("(k p) i -> p k i", p=P)).then_inc(wgu_in, 16)
            sp.dma_start(wd_raw[:, :, :], t["w_downT"].rearrange("(j p) d -> p j d", p=P))\
              .then_inc(wd_in, 16)
            with sp.Fori(0, B) as n:
                sp.wait_ge(partsT_copied, 1 + (n + 1) * TPB)
                sp.dma_start(t["qk_parts"][bass.ds(n, 1)].rearrange("b m p s -> p (b m) s"),
                             stage[:, :, :]).then_inc(stored, 16)
            sp.wait_ge(stored, 1 + B * 16)

        @block.gpsimd
        def _(pool):
            pool.memset(v_pad[:, :, :, :], 0.0).then_inc(v_clear, 1)
            pool.wait_ge(v_clear, 1)
            pool.memset(v_pad[:, :, :, HD:HD + 1], 1.0).then_inc(v_clear, 1)

        @block.scalar
        def _(act):
            prime(act, qkv_copied, partsT_copied)
            act.dma_start(su_ug[:, :], t["su_ug"].rearrange("(k p) -> p k", p=P),
                          allow_slow_non_contiguous=True).then_inc(scale_in, 16)
            act.dma_start(su_dp[:, :], t["su_dp"].rearrange("(k p) -> p k", p=P),
                          allow_slow_non_contiguous=True).then_inc(scale_in, 16)
            act.dma_start(ws_ug[:, :, :], t["ws_ug"].rearrange("(m i p) -> p m i", p=P, m=2),
                          allow_slow_non_contiguous=True).then_inc(scale_in, 16)
            act.dma_start(ws_dp[:, :], t["ws_dp"].partition_broadcast(P)).then_inc(scale_in, 16)
            for b in range(B):
                act.dma_start(x_sb[:, TPB * b:TPB * (b + 1), :],
                              t["x"][T * b:T * (b + 1), :].rearrange("(i p) d -> p i d", p=P))\
                   .then_inc(x_in[b], 16)
            act.dma_start(ident[:, :], t["ident"]).then_inc(const_in, 16)
            act.dma_start(identb[:, :], t["identb"]).then_inc(const_in, 16)
            act.dma_start(rope[:, :, :, :], t["rope"]).then_inc(const_in, 16)
            for c0, c1, name in ((0, H0 * HD, "wqT"), (H0 * HD, QK, "wkT"), (QK, QKV, "wvT")):
                act.dma_start(w_qkv[:, :, c0:c1],
                              t[name].rearrange("(k p) i -> p k i", p=P)).then_inc(wqkv_in, 16)
            act.wait_ge(scale_in, 64)
            for m in range(KD):
                for w in range(2):
                    for c in range(2):
                        s = (m * 2 + w) * 2 + c
                        act.wait_ge(had_ready, s + 1)
                        nc.scalar.activation(w_gu[:, m, w, c * 512:(c + 1) * 512], ps_gu[:, s % 4, :],
                                             ACT.Copy, scale=su_ug[:, m:m + 1]).then_inc(had_copied, 1)
            act.wait_ge(down_had, 1)
            nc.scalar.activation(wd_a[:, :, :].rearrange("p (c a) d -> p c (a d)", c=4),
                                 ps_gu[:, :, :], ACT.Copy).then_inc(down_copied, 1)
            act.wait_ge(v_clear, 2)
            with act.Fori(0, B) as n:
                act.wait_ge(var_ready, n + 1)
                nc.scalar.activation(std[:, :], var[:, :], ACT.Sqrt).then_inc(std_ready, 1)
                act.wait_ge(gu_ready, 1 + n * NI0)
                for i in range(TPB):
                    act.wait_ge(xT_ready, 1 + n * TPB + i + 1)
                    nc.scalar.activation(xnT[:, :, i * P:(i + 1) * P],
                                         ps_x[:, i % 2, 0:D].rearrange("p (k c) -> p k c", k=KD),
                                         ACT.Copy).then_inc(xT_copied, 1)
                act.wait_ge(parts_ready, 1 + n * TPB * 2)
                for i in range(TPB):
                    act.wait_ge(qkv_ready, n * TPB + i + 1)
                    nc.scalar.activation(qk[:, i, :], ps_qkv[:, 0:QK], ACT.Copy).then_inc(qkv_copied, 1)
                    nc.scalar.activation(
                        v_pad[:, bass.ds(n * TPB + i, 1), :, 0:HD].rearrange("p a g d -> p (a g) d"),
                        ps_qkv[:, QK:QKV].rearrange("p (g d) -> p g d", d=HD),
                        ACT.Copy).then_inc(qkv_copied, 1)

                def copy_parts(i):
                    act.wait_ge(partsT_ready, 1 + n * TPB + i + 1)
                    nc.scalar.activation(stage[:, :, i * P:(i + 1) * P], ps_parts[:, :, :],
                                         ACT.Copy).then_inc(partsT_copied, 1)

                for i in range(NI0):
                    act.wait_ge(gu_ready, 1 + n * NI0 + i + 1)
                    if i >= 2:
                        act.wait_ge(h_ready, 1 + n * NI0 + i - 1)
                    else:
                        act.wait_ge(h_ready, 1 + n * NI0)
                    nc.scalar.activation(sg[:, i % 2, :], ps_gu[:, 2 * (i % 2), :], ACT.Silu,
                                         scale=ws_ug[:, 1, i:i + 1]).then_inc(silu_ready, 1)
                    if i == 0:
                        act.wait_ge(stored, 1 + n * 16)
                    if 1 <= i <= TPB:
                        copy_parts(i - 1)

        @block.vector
        def _(dve):
            prime(dve, parts_ready, h_ready, added)
            ch = Chain(dve, dve_step)
            dve.wait_ge(down_copied, 1)
            src, dst = wd_a, wd_b
            for h in (1, 2, 4):
                a = src[:, :, :].rearrange("p (u r h) d -> p u r (h d)", r=2, h=h)
                o = dst[:, :, :].rearrange("p (u r h) d -> p u r (h d)", r=2, h=h)
                ch.did(nc.vector.tensor_tensor(o[:, :, 0, :], a[:, :, 0, :], a[:, :, 1, :], ALU.add))
                ch.step(nc.vector.tensor_tensor(o[:, :, 1, :], a[:, :, 0, :], a[:, :, 1, :], ALU.subtract))
                src, dst = dst, src
            dve.wait_ge(scale_in, 64)
            for j in range(NI0):
                ins = nc.vector.scalar_tensor_tensor(w_down[:, j, :], src[:, j, :], su_dp[:, j:j + 1],
                                                     ws_dp[:, :], ALU.mult, ALU.mult)
            ins.then_inc(w_ready, 1)
            for b in range(B):
                dve.wait_ge(x_in[b], 16)
            dve.wait_ge(const_in, 48)
            PER = 2 * TPB + 1 + TPB * 10
            with dve.Fori(0, B) as n:
                ch.enter(n, PER)
                apart(dve, waits)
                for i in range(TPB):
                    xi = x_sb[:, bass.ds(n * TPB + i, 1), :].rearrange("p a d -> p (a d)")
                    ch.did(nc.vector.bn_stats(stats[:, i, :], xi))
                ch.last()
                apart(dve, waits)
                for i in range(TPB):
                    ch.did(nc.vector.bn_aggr(mv[:, i, :], stats[:, i, :]))
                ch.last()
                nc.vector.tensor_scalar(var[:, :], mv[:, :, 1], EPS, None, ALU.add).then_inc(var_ready, 1)
                dve.wait_ge(std_ready, n + 1)
                ch.step(nc.vector.reciprocal(rstd[:, :], std[:, :]))
                dve.wait_ge(xT_ready, 1 + n * TPB)
                for i in range(TPB):
                    xi = x_sb[:, bass.ds(n * TPB + i, 1), :].rearrange("p a d -> p (a d)")
                    nc.vector.tensor_scalar(xn[:, i, :], xi, mv[:, i, 0:1], rstd[:, i:i + 1],
                                            ALU.subtract, ALU.mult).then_inc(xn_ready, 1)

                def rotate(i):
                    dve.wait_ge(qkv_copied, 1 + (n * TPB + i + 1) * 2)
                    q3 = qk[:, i, :].rearrange("p (h c) -> p h c", c=HD)
                    q4 = qk[:, i, :].rearrange("p (h c r) -> p h c r", c=HD // 2, r=2)
                    b4 = rot_b[:, :].rearrange("p (h c r) -> p h c r", c=HD // 2, r=2)
                    cos = rope[:, i, 0:1, :].to_broadcast([P, QK // HD, HD])
                    sin = rope[:, i, 1:2, :].rearrange("p a (c r) -> p a c r", r=2)
                    ch.did(nc.vector.tensor_tensor(rot[:, :].rearrange("p (h c) -> p h c", c=HD),
                                                   q3, cos, ALU.mult))
                    for r in range(2):
                        ch.did(nc.vector.tensor_tensor(
                            b4[:, :, :, r], q4[:, :, :, 1 - r],
                            sin[:, :, :, r].to_broadcast([P, QK // HD, HD // 2]), ALU.mult))
                    ch.last()
                    ch.step(nc.vector.tensor_tensor(rot[:, :], rot[:, :], rot_b[:, :], ALU.add))
                    if i >= 2:
                        dve.wait_ge(partsT_ready, 1 + n * TPB + i - 1)
                    else:
                        dve.wait_ge(partsT_ready, 1 + n * TPB)
                    pq, pk = parts_q[:, i % 2], parts_k[:, i % 2]
                    nq = H0 * HD
                    ch.did(nc.vector.tensor_copy(pq[:, 0, :], rot[:, 0:nq]))
                    ch.step(nc.vector.tensor_copy(pk[:, 0, :], rot[:, nq:]))
                    ch.did(nc.vector.tensor_tensor(rest[:, 0:nq], rot[:, 0:nq], pq[:, 0, :], ALU.subtract))
                    ch.step(nc.vector.tensor_tensor(rest[:, nq:], rot[:, nq:], pk[:, 0, :], ALU.subtract))
                    ch.did(nc.vector.tensor_copy(pq[:, 1, :], rest[:, 0:nq]))
                    ch.step(nc.vector.tensor_copy(pk[:, 1, :], rest[:, nq:]))
                    nc.vector.tensor_tensor(pq[:, 2, :], rest[:, 0:nq], pq[:, 1, :], ALU.subtract)\
                      .then_inc(parts_ready, 1)
                    nc.vector.tensor_tensor(pk[:, 2, :], rest[:, nq:], pk[:, 1, :], ALU.subtract)\
                      .then_inc(parts_ready, 1)

                def gate(i):
                    dve.wait_ge(silu_ready, n * NI0 + i + 1)
                    if i == 0:
                        dve.wait_ge(down_ready, 1 + n * TPB)
                    nc.vector.scalar_tensor_tensor(hT[:, i, :], ps_gu[:, 2 * (i % 2) + 1, :],
                                                   ws_ug[:, 0, i:i + 1], sg[:, i % 2, :],
                                                   ALU.mult, ALU.mult).then_inc(h_ready, 1)

                rotate(0)
                rotate(1)
                gate(0)
                rotate(2)
                gate(1)
                rotate(3)
                for i in range(2, NI0):
                    gate(i)
                for i in range(TPB):
                    xi = x_sb[:, bass.ds(n * TPB + i, 1), :].rearrange("p a d -> p (a d)")
                    dve.wait_ge(down_ready, 1 + n * TPB + i + 1)
                    nc.vector.tensor_tensor(xi, xi, ps_x[:, i % 2, 0:D], ALU.add).then_inc(added, 1)
                dve.wait_ge(added, 1 + (n + 1) * TPB)
                ch.leave(B, PER)

        @block.tensor
        def _(pe):
            prime(pe, gu_ready, xT_ready, partsT_ready, down_ready)
            pe.wait_ge(had_in, 16)
            pe.wait_ge(wgu_in, 32)
            for m in range(KD):
                for w in range(2):
                    for c in range(2):
                        s = (m * 2 + w) * 2 + c
                        if s >= 4:
                            pe.wait_ge(had_copied, s - 3)
                        for k in range(KD):
                            ins = nc.tensor.matmul(ps_gu[:, s % 4, :], had[:, m & k, :],
                                                   w_raw[:, k, w, c * 512:(c + 1) * 512],
                                                   start=(k == 0), stop=(k == KD - 1))
                        ins.then_inc(had_ready, 1)
            pe.wait_ge(wd_in, 16)
            pe.wait_ge(had_copied, 8)
            wd = wd_raw[:, :, :].rearrange("p (c a) d -> p c (a d)", c=4)
            for c in range(4):
                ins = nc.tensor.matmul(ps_gu[:, c, :], had[:, 2, :], wd[:, c, :], start=True, stop=True)
            ins.then_inc(down_had, 1)
            pe.wait_ge(down_copied, 1)
            pe.wait_ge(const_in, 48)
            pe.wait_ge(wqkv_in, 48)
            with pe.Fori(0, B) as n:
                pe.wait_ge(added, 1 + n * TPB)
                for i in range(TPB):
                    pe.wait_ge(xn_ready, n * TPB + i + 1)
                    if i >= 2:
                        pe.wait_ge(xT_copied, n * TPB + i - 1)
                    for k in range(KD):
                        ins = nc.tensor.transpose(ps_x[:, i % 2, k * P:(k + 1) * P],
                                                  xn[:, i, k * P:(k + 1) * P], ident[:, :])
                    ins.then_inc(xT_ready, 1)
                for i in range(TPB):
                    pe.wait_ge(xT_copied, n * TPB + i + 1)
                    pe.wait_ge(qkv_copied, 1 + (n * TPB + i) * 2)
                    for k in range(KD):
                        ins = nc.tensor.matmul(ps_qkv[:, 0:QKV], xnT[:, k, i * P:(i + 1) * P],
                                               w_qkv[:, k, :], start=(k == 0), stop=(k == KD - 1))
                    ins.then_inc(qkv_ready, 1)

                def parts_T(i):
                    pe.wait_ge(parts_ready, 1 + (n * TPB + i + 1) * 2)
                    pe.wait_ge(partsT_copied, 1 + n * TPB + i)
                    for s in range(NP_):
                        for m in range(2):
                            nc.tensor.transpose(ps_parts[:, s * 2 + m, :],
                                                parts_q[:, i % 2, s, m * P:(m + 1) * P], identb[:, :])
                    for s in range(2):
                        ins = nc.tensor.transpose(
                            ps_parts[:, NP_ * 2 + s, :],
                            parts_k[:, i % 2, s:s + 2, :].rearrange("p s c -> p (s c)"), identb[:, :])
                    ins.then_inc(partsT_ready, 1)

                for i in range(NI0):
                    if i >= 2:
                        pe.wait_ge(h_ready, 1 + n * NI0 + i - 1)
                    else:
                        pe.wait_ge(h_ready, 1 + n * NI0)
                    for w in range(2):
                        for k in range(KD):
                            ins = nc.tensor.matmul(ps_gu[:, 2 * (i % 2) + w, :],
                                                   w_gu[:, k, w, i * P:(i + 1) * P], xnT[:, k, :],
                                                   start=(k == 0), stop=(k == KD - 1))
                    ins.then_inc(gu_ready, 1)
                    if 1 <= i <= TPB:
                        parts_T(i - 1)
                pe.wait_ge(w_ready, 1)
                pe.wait_ge(h_ready, 1 + (n + 1) * NI0)
                for i in range(TPB):
                    if i >= 2:
                        pe.wait_ge(added, 1 + n * TPB + i - 1)
                    for k in range(NI0):
                        ins = nc.tensor.matmul(ps_x[:, i % 2, 0:D], hT[:, k, i * P:(i + 1) * P],
                                               w_down[:, k, :], start=(k == 0), stop=(k == NI0 - 1))
                    ins.then_inc(down_ready, 1)


def layer0_attention(nc, t, v_pad, yn):
    ctx = ExitStack()
    with ctx:
        ident = sbuf(ctx, nc, "b_ident", [P, P])
        identb = sbuf(ctx, nc, "b_identb", [P, P], BF16)
        causal = sbuf(ctx, nc, "b_causal", [P, P], BF16)
        mask = sbuf(ctx, nc, "b_mask", [P, T])
        masked = sbuf(ctx, nc, "b_masked", [P, 3, T], BF16)
        qT = [sbuf(ctx, nc, f"b_qT{i}", [SROWS, HKV, REP, T], BF16) for i in range(2)]
        kT = [sbuf(ctx, nc, f"b_kT{i}", [SROWS, HKV, T], BF16) for i in range(3)]
        headmax = sbuf(ctx, nc, "b_headmax", [P, HKV, TPB])
        rowmax = sbuf(ctx, nc, "b_rowmax", [P, HKV, REP, TPB])
        negmaxT = sbuf(ctx, nc, "b_negmaxT", [P, P])
        m_rest = sbuf(ctx, nc, "b_m_rest", [P, P])
        m_parts = sbuf(ctx, nc, "b_m_parts", [P, NP_, P], BF16)
        probs = sbuf(ctx, nc, "b_probs", [P, HKV, 1280])
        y_raw = sbuf(ctx, nc, "b_y_raw", [P, 2, T])
        rden = sbuf(ctx, nc, "b_rden", [P, TPB, 4])

        ps_s = psum(ctx, nc, "b_ps_s", [P, 3, 512])
        ps_e = psum(ctx, nc, "b_ps_e", [P, 3, 512])
        ps_y = psum(ctx, nc, "b_ps_y", [P, 512])
        ps_t = psum(ctx, nc, "b_ps_t", [P, TPB, P])

        (const_in, mask_in, waits, step, max_ready, max_done, max_kept, heads_done, mT_ready, m_split, m_in,
         st_ready, exp_done, pv_done, y_copied, yT_ready, norm_done) = sems(
            ctx, nc, *("b_" + s for s in (
                "const_in mask_in waits step max_ready max_done max_kept heads_done mT_ready m_split m_in "
                "st_ready exp_done pv_done y_copied yT_ready norm_done").split()))
        q_loaded = sems(ctx, nc, "b_q_loaded0", "b_q_loaded1")
        k_loaded = sems(ctx, nc, "b_k_loaded0", "b_k_loaded1", "b_k_loaded2")
        block = ctx.enter_context(nc.Block())
        QDMA = KDMA = NC_ + 1
        UNITS = [[(0, 0)], [(3, 0), (1, P)], [(2, 0)]]
        UCOL = [0, 512, 1024, 1280]
        MUNITS = [[(3, 0)], [(2, 0), (0, 3 * P)], [(1, 0)]]

        @block.sync
        def _(sp):
            sp.dma_start(ident[:, :], t["ident"]).then_inc(const_in, 16)
            sp.dma_start(identb[:, :], t["identb"]).then_inc(const_in, 16)
            sp.dma_start(causal[:, :], t["causal"]).then_inc(const_in, 16)
            sp.dma_start(mask[:, :], t["mask"]).then_inc(mask_in, 16)

            def load_k(b):
                k = kT[b % 3]
                sp.dma_start(k[MROW:SROWS],
                             t["pad"][1:2].rearrange("a p s -> p a s")
                             .to_broadcast([SROWS - MROW, HKV, T])).then_inc(k_loaded[b % 3], 16)
                for i in range(NP_):
                    for j in range(NP_):
                        r = (i * NP_ + j) * HD
                        slot, row = ((6, 0), (7, 0), (7, 64))[j]
                        sp.dma_start(k[r:r + HD],
                                     t["qk_parts"][b, slot, row:row + HKV * HD]
                                     .rearrange("(h d) s -> d h s", d=HD)).then_inc(k_loaded[b % 3], 16)

            def load_q(b, h):
                q, sem = qT[b % 2], q_loaded[b % 2]
                if b // 2 * REP + h:
                    sp.wait_ge(sem, (b // 2 * REP + h) * QDMA * 16)
                if b >= 2:
                    sp.wait_ge(pv_done, 1 + ((b - 2) * REP + h + 1) * 2)
                sp.dma_start(q[MROW:SROWS, :, h, :],
                             t["pad"][0:1].rearrange("a p s -> p a s")
                             .to_broadcast([SROWS - MROW, HKV, T])).then_inc(sem, 16)
                for i in range(NP_):
                    for j in range(NP_):
                        r = (i * NP_ + j) * HD
                        sp.dma_start(q[r:r + HD, :, h, :],
                                     t["qk_parts"][b, 2 * i:2 * i + 2]
                                     .rearrange("m (g h d) s -> h d (m g) s", d=HD, h=REP)[h])\
                          .then_inc(sem, 16)

            def load_maximum(b):
                sp.wait_ge(m_split, b + 1)
                for s in range(NP_):
                    sp.dma_start(qT[b % 2][MROW + s:MROW + s + 1].rearrange("p g r s -> p (g r s)"),
                                 m_parts[:, s, :]).then_inc(m_in, 16)

            load_k(0)
            for b in range(B):
                for h in range(REP - 1):
                    load_q(b, h)
                if b >= 1:
                    load_maximum(b - 1)
                load_q(b, REP - 1)
                if b + 1 < B:
                    load_k(b + 1)
            load_maximum(B - 1)

        @block.scalar
        def _(act):
            prime(act, exp_done, y_copied)
            for b in range(B):
                with act.Fori(0, REP) as h:
                    hi = h + b * REP

                    def copy_y(G):
                        act.wait_ge(pv_done, 1 + hi * 2 + G + 1)
                        act.wait_ge(yT_ready, 1 + hi * 2)
                        nc.scalar.activation(y_raw[:, G, :], ps_y[:, :], ACT.Copy).then_inc(y_copied, 1)

                    act.wait_ge(pv_done, 1 + hi * 2)
                    for g in range(HKV):
                        gi = hi * HKV + g
                        for u in range(3):
                            act.wait_ge(st_ready, gi * 3 + u + 1)
                            n = UCOL[u + 1] - UCOL[u]
                            nc.scalar.activation(probs[:, g, UCOL[u]:UCOL[u + 1]], ps_e[:, u, 0:n],
                                                 ACT.Exp, scale=SCALE0).then_inc(exp_done, 1)
                        if g == 6:
                            copy_y(0)
                    copy_y(1)

        @block.vector
        def _(dve):
            prime(dve, norm_done, max_done, max_kept)
            dve.wait_ge(mask_in, 16)
            for ph in range(B + 1):
                with dve.Fori(0, REP) as h:
                    hi = h + (ph - 1) * REP if ph else h

                    def normalize(G):
                        dve.wait_ge(yT_ready, 1 + hi * 2 + G + 1)
                        y = ps_t[:, :, :].rearrange("p a (j c) -> p a j c", c=VW)
                        nc.vector.reciprocal(rden[:, :, :], y[:, :, :, HD]).then_inc(step, 1)
                        dve.wait_ge(step, hi * 2 + G + 1)
                        b = ph - 1
                        o = yn[:, b * TPB:(b + 1) * TPB, :]\
                            .rearrange("p a (G j r d) -> p a G j r d", G=2, j=4, r=REP)
                        o = o[:, :, G, :, bass.ds(h, 1), :].rearrange("p a j r d -> p a j (r d)")
                        nc.vector.tensor_tensor(o, y[:, :, :, 0:HD],
                                                rden[:, :, :].rearrange("p a (j c) -> p a j c", c=1)
                                                .to_broadcast([P, TPB, 4, HD]),
                                                ALU.mult).then_inc(norm_done, 1)

                    for g in range(HKV):
                        if ph < B:
                            gi = (h + ph * REP) * HKV + g
                            for u in range(3):
                                dve.wait_ge(max_ready, gi * 3 + u + 1)
                                if g == 0 and u == 0:
                                    dve.wait_ge(max_kept, 1 + h + ph * REP)
                                dve.wait_ge(max_done, 1 + gi * 3 + (u - 2 if g else 0))
                                apart(dve, waits)
                                for q, c in MUNITS[u]:
                                    w = (q + 1) * P
                                    ins = nc.vector.tensor_tensor_reduce(
                                        masked[:, u, c:c + w],
                                        ps_s[:, u, c:c + w],
                                        mask[:, T - w:T], 1.0, -3e38,
                                        ALU.add, ALU.max, headmax[:, g, q:q + 1])
                                ins.then_inc(max_done, 1)
                        if ph and g == 6:
                            normalize(0)
                    if ph:
                        normalize(1)
                    if ph < B:
                        dve.wait_ge(max_done, 1 + (h + ph * REP + 1) * HKV * 3)
                        if ph:
                            dve.wait_ge(mT_ready, ph)
                        nc.vector.tensor_copy(
                            rowmax[:, :, bass.ds(h, 1), :].rearrange("p g r a -> p g (r a)"),
                            headmax[:, :, :]).then_inc(max_kept, 1)
                if ph < B:
                    dve.wait_ge(mT_ready, ph + 1)
                    base = ph * 5
                    nc.vector.tensor_scalar(negmaxT[:, :], ps_t[:, 0, :], -1.0, None, ALU.mult)\
                      .then_inc(heads_done, 1)
                    dve.wait_ge(heads_done, base + 1)
                    if ph:
                        dve.wait_ge(m_in, ph * 48)
                    nc.vector.tensor_copy(m_parts[:, 0, :], negmaxT[:, :]).then_inc(heads_done, 1)
                    dve.wait_ge(heads_done, base + 2)
                    nc.vector.tensor_tensor(m_rest[:, :], negmaxT[:, :], m_parts[:, 0, :],
                                            ALU.subtract).then_inc(heads_done, 1)
                    dve.wait_ge(heads_done, base + 3)
                    nc.vector.tensor_copy(m_parts[:, 1, :], m_rest[:, :]).then_inc(heads_done, 1)
                    dve.wait_ge(heads_done, base + 4)
                    nc.vector.tensor_tensor(m_parts[:, 2, :], m_rest[:, :], m_parts[:, 1, :],
                                            ALU.subtract).then_inc(heads_done, 1)
                    dve.wait_ge(heads_done, base + 5)
                    nc.vector.engine_nop().then_inc(m_split, 1)

        @block.tensor
        def _(pe):
            prime(pe, pv_done, yT_ready)
            pe.wait_ge(const_in, 48)
            for ph in range(B + 1):
                if ph < B:
                    pe.wait_ge(k_loaded[ph % 3], KDMA * 16 * (ph // 3 + 1))
                if ph:
                    pe.wait_ge(m_in, 48 * ph)
                with pe.Fori(0, REP) as h:
                    if ph < B:
                        pe.wait_ge(q_loaded[ph % 2], (h + ph // 2 * REP + 1) * QDMA * 16)
                    mi = h + ph * REP
                    hi = h + (ph - 1) * REP if ph else h

                    def head(x, g, c0, c1):
                        return x[:, g, bass.ds(h, 1), c0:c1].rearrange("p r s -> p (r s)")

                    def max_scores(g, u):
                        q, k = qT[ph % 2], kT[ph % 3]
                        pe.wait_ge(max_done, 1 + ((mi * HKV + g) * 3 + (u - 2 if g else 0)))
                        out = ps_s[:, u, :]
                        for a, c in MUNITS[u]:
                            ins = nc.tensor.matmul(out[:, c:c + (a + 1) * P],
                                                   head(q, g, a * P, (a + 1) * P),
                                                   k[:, g, 0:(a + 1) * P], start=True, stop=True,
                                                   skip_group_check=True)
                        ins.then_inc(max_ready, 1)

                    def key_scores(g):
                        q, k = qT[(ph - 1) % 2], kT[(ph - 1) % 3]
                        gi = hi * HKV + g
                        for u in range(3):
                            pe.wait_ge(exp_done, 1 + (gi * 3 + (u - 2 if g else 0)))
                            for s, c in UNITS[u]:
                                nc.tensor.matmul(ps_e[:, u, c:c + T - s * P],
                                                 k[:, g, s * P:(s + 1) * P], head(q, g, s * P, T),
                                                 start=True, stop=False, skip_group_check=True)
                                ins = nc.tensor.matmul(ps_e[:, u, c:c + P], identb[:, :],
                                                       causal[:, :], start=False, stop=True,
                                                       skip_group_check=True)
                            ins.then_inc(st_ready, 1)

                    def values(G, u):
                        if u == 0:
                            pe.wait_ge(y_copied, 1 + hi * 2 + G)
                        pe.wait_ge(exp_done, 1 + (hi * HKV + 4 * G + 3) * 3 + u + 1)
                        for s, c in UNITS[u]:
                            for j in range(4):
                                ins = nc.tensor.matmul(
                                    ps_y[VW * j:VW * (j + 1), s * P:T],
                                    v_pad[:, (ph - 1) * TPB + s, 4 * G + j, :],
                                    probs[:, 4 * G + j, UCOL[u] + c:UCOL[u] + c + T - s * P],
                                    start=(s == 0), stop=(u == 2), skip_group_check=True)
                        if u == 2:
                            ins.then_inc(pv_done, 1)

                    def transposes(G):
                        pe.wait_ge(y_copied, 1 + hi * 2 + G + 1)
                        pe.wait_ge(norm_done, 1 + hi * 2 + G)
                        for a in range(TPB):
                            ins = nc.tensor.transpose(ps_t[:, a, :], y_raw[:, G, a * P:(a + 1) * P],
                                                      ident[:, :])
                        ins.then_inc(yT_ready, 1)

                    maxima = [(g, u) for g in range(HKV) for u in range(3)] if ph < B else []

                    def fill(upto):
                        while maxima and maxima[0] <= upto:
                            max_scores(*maxima.pop(0))

                    for g in range(HKV):
                        if ph:
                            key_scores(g)
                            if g == 7:
                                transposes(0)
                            fill((g, 0))
                            if g in (4, 5, 6):
                                values(0, g - 4)
                        fill((g, 1 if g < HKV - 1 else 0))
                    if ph:
                        values(1, 0)
                        fill((HKV - 1, 1))
                        values(1, 1)
                        values(1, 2)
                    fill((HKV - 1, 2))
                    if ph:
                        transposes(1)
                if ph < B:
                    pe.wait_ge(max_kept, 1 + (ph + 1) * REP)
                    if ph:
                        pe.wait_ge(norm_done, 1 + ph * REP * 2)
                    nc.tensor.transpose(ps_t[:, 0, :], rowmax[:, :, :, :].rearrange("p g r a -> p (g r a)"),
                                        ident[:, :]).then_inc(mT_ready, 1)


def layer1_front(nc, t, x_sb, yn, qkv1, logits):
    ctx = ExitStack()
    with ctx:
        ident = sbuf(ctx, nc, "c_ident", [P, P])
        w_o = sbuf(ctx, nc, "c_w_o", [P, KD, D])
        w_r = sbuf(ctx, nc, "c_w_r", [P, KD, NE])
        w_qkv = sbuf(ctx, nc, "c_w_qkv", [P, KD, 3 * D])
        y_cur = sbuf(ctx, nc, "c_y_cur", [P, 2, D])
        yT = sbuf(ctx, nc, "c_yT", [P, 2, KD, P])
        xn = sbuf(ctx, nc, "c_xn", [P, 2, D])
        xT = sbuf(ctx, nc, "c_xT", [P, 2, KD, P])
        stats = sbuf(ctx, nc, "c_stats", [P, 6])
        mv = sbuf(ctx, nc, "c_mv", [P, 2])
        var = sbuf(ctx, nc, "c_var", [P, 1])
        std = sbuf(ctx, nc, "c_std", [P, 1])
        rstd = sbuf(ctx, nc, "c_rstd", [P, 1])

        ps_yT = psum(ctx, nc, "c_ps_yT", [P, 512])
        ps_o = psum(ctx, nc, "c_ps_o", [P, 512])
        ps_xT = psum(ctx, nc, "c_ps_xT", [P, 512])
        ps_r = psum(ctx, nc, "c_ps_r", [P, 512])
        ps_qkv = psum(ctx, nc, "c_ps_qkv", [P, 2, 2, 512])

        (w_in, step, y_ready, yT_ready, yT_copied, o_ready, var_ready, std_ready, xn_ready,
         xn_stored, xT_ready, xT_copied, r_ready, r_copied, qkv_ready, qkv_copied, waits) = sems(
            ctx, nc, *("c_" + s for s in (
                "w_in step y_ready yT_ready yT_copied o_ready var_ready std_ready xn_ready "
                "xn_stored xT_ready xT_copied r_ready r_copied qkv_ready qkv_copied waits").split()))
        block = ctx.enter_context(nc.Block())

        def tiles(eng, body):
            with eng.Fori(0, NT // 2 - 1) as i:
                for r in range(2):
                    body(i * 2 + r, r, True)
            body(NT - 2, 0, True)
            body(NT - 1, 1, False)

        def tile_of(x, n):
            return x[:, bass.ds(n, 1), :].rearrange("p a d -> p (a d)")

        @block.sync
        def _(sp):
            prime(sp, xn_stored)
            sp.dma_start(ident[:, :], t["ident"]).then_inc(w_in, 16)
            for w, name in ((w_o, "woT"), (w_r, "routerT"), (w_qkv, "w_qkv1T")):
                sp.dma_start(w[:, :, :], t[name].rearrange("(k p) i -> p k i", p=P)).then_inc(w_in, 16)

            def store(n, r, more):
                sp.wait_ge(xn_ready, n + 1)
                sp.dma_start(t["rows"][0:TOK].rearrange("(n p) d -> n p d", p=P)[bass.ds(n, 1), :, 0:D]
                             .rearrange("a p d -> p (a d)"), xn[:, r, :])\
                  .then_inc(xn_stored, 16)

            tiles(sp, store)
            sp.wait_ge(xn_stored, 1 + NT * 16)

        @block.gpsimd
        def _(pool):
            def copy(n, r, more):
                pool.wait_ge(yT_ready, 1 + (n + (r - 1) if r else n))
                nc.gpsimd.tensor_copy(y_cur[:, r, :], tile_of(yn, n)).then_inc(y_ready, 1)

            tiles(pool, copy)

        @block.scalar
        def _(act):
            prime(act, yT_copied, xT_copied, r_copied, qkv_copied)
            def copy_yT(n, r):
                act.wait_ge(yT_ready, 1 + n + 1)
                nc.scalar.activation(yT[:, r], ps_yT[:, 0:D].rearrange("p (k c) -> p k c", k=KD),
                                     ACT.Copy).then_inc(yT_copied, 1)

            def root(n):
                act.wait_ge(var_ready, 1 + n + 1)
                nc.scalar.activation(std[:, :], var[:, :], ACT.Sqrt).then_inc(std_ready, 1)

            copy_yT(0, 0)
            root(0)

            def tile(n, r, more):
                if more:
                    copy_yT(n + 1, 1 - r)
                act.wait_ge(xT_ready, 1 + n + 1)
                nc.scalar.activation(xT[:, r], ps_xT[:, 0:D].rearrange("p (k c) -> p k c", k=KD),
                                     ACT.Copy).then_inc(xT_copied, 1)
                if more:
                    root(n + 1)
                act.wait_ge(r_ready, n + 1)
                nc.scalar.activation(tile_of(logits, n), ps_r[:, 0:NE], ACT.Copy).then_inc(r_copied, 1)
                act.wait_ge(qkv_ready, n + 1)
                nc.scalar.activation(tile_of(qkv1, n).rearrange("p (a c) -> p a c", a=2),
                                     ps_qkv[:, r, :, 0:384], ACT.Copy).then_inc(qkv_copied, 1)

            tiles(act, tile)

        @block.vector
        def _(dve):
            prime(dve, var_ready)
            ch = Chain(dve, step)

            def tile(n, r):
                dve.wait_ge(o_ready, n + 1)
                x = tile_of(x_sb, n)
                ch.step(nc.vector.tensor_tensor(x, x, ps_o[:, 0:D], ALU.add))
                apart(dve, waits)
                ch.step(nc.vector.bn_stats(stats[:, :], x))
                apart(dve, waits)
                ch.step(nc.vector.bn_aggr(mv[:, :], stats[:, :]))
                nc.vector.tensor_scalar(var[:, :], mv[:, 1:2], EPS, None, ALU.add).then_inc(var_ready, 1)
                dve.wait_ge(std_ready, n + 1)
                ch.step(nc.vector.reciprocal(rstd[:, :], std[:, :]))
                dve.wait_ge(xT_ready, 1 + (n - 1 if r else n))
                dve.wait_ge(xn_stored, 1 + ((n - 1 if r else n) * 16))
                nc.vector.tensor_scalar(xn[:, r, :], x, mv[:, 0:1], rstd[:, :],
                                        ALU.subtract, ALU.mult).then_inc(xn_ready, 1)

            with dve.Fori(0, NT // 2) as i:
                ch.enter(i, 8)
                for r in range(2):
                    tile(i * 2 + r, r)
                ch.leave(NT // 2, 8)

        @block.tensor
        def _(pe):
            prime(pe, yT_ready, xT_ready)
            pe.wait_ge(w_in, 64)

            def output(n, r):
                pe.wait_ge(y_ready, n + 1)
                pe.wait_ge(yT_copied, 1 + n)
                for k in range(KD):
                    ins = nc.tensor.transpose(ps_yT[:, k * P:(k + 1) * P],
                                              y_cur[:, r, k * P:(k + 1) * P], ident[:, :])
                ins.then_inc(yT_ready, 1)
                pe.wait_ge(yT_copied, 1 + n + 1)
                pe.wait_ge(var_ready, 1 + n)
                for k in range(KD):
                    ins = nc.tensor.matmul(ps_o[:, 0:D], yT[:, r, k, :], w_o[:, k, :],
                                           start=(k == 0), stop=(k == KD - 1))
                ins.then_inc(o_ready, 1)

            output(0, 0)

            def tile(n, r, more):
                if more:
                    output(n + 1, 1 - r)
                pe.wait_ge(xn_ready, n + 1)
                pe.wait_ge(xT_copied, 1 + n)
                for k in range(KD):
                    ins = nc.tensor.transpose(ps_xT[:, k * P:(k + 1) * P],
                                              xn[:, r, k * P:(k + 1) * P], ident[:, :])
                ins.then_inc(xT_ready, 1)
                pe.wait_ge(xT_copied, 1 + n + 1)
                pe.wait_ge(r_copied, 1 + n)
                for k in range(KD):
                    ins = nc.tensor.matmul(ps_r[:, 0:NE], xT[:, r, k, :], w_r[:, k, :],
                                           start=(k == 0), stop=(k == KD - 1))
                ins.then_inc(r_ready, 1)
                pe.wait_ge(qkv_copied, 1 + (n - 1 if r else n))
                for c in range(2):
                    for k in range(KD):
                        ins = nc.tensor.matmul(ps_qkv[:, r, c, 0:384], xT[:, r, k, :],
                                               w_qkv[:, k, c * 384:(c + 1) * 384],
                                               start=(k == 0), stop=(k == KD - 1))
                ins.then_inc(qkv_ready, 1)

            tiles(pe, tile)


def layer1_routing(nc, t, logits, block_expert, expert_f, inv):
    ctx = ExitStack()
    with ctx:
        sums = sbuf(ctx, nc, "d_sums", [P, 2, P], BF16)
        order = sbuf(ctx, nc, "d_order", [P, 2, NG, NG])
        bias = sbuf(ctx, nc, "d_bias", [P, NE])
        tok_id = sbuf(ctx, nc, "d_tok_id", [P, NT])
        iota = sbuf(ctx, nc, "d_iota", [P, NLOAD], FP16)
        blk_id = sbuf(ctx, nc, "d_blk_id", [P, 2])
        pad_id = sbuf(ctx, nc, "d_pad_id", [P, 1])
        zeros = sbuf(ctx, nc, "d_zeros", [P, TOK * D // P])
        val = sbuf(ctx, nc, "d_val", [P, NT, NE])
        v8 = sbuf(ctx, nc, "d_v8", [P, NT, 8])
        w = sbuf(ctx, nc, "d_w", [P, NT, NE])
        is_pad = sbuf(ctx, nc, "d_is_pad", [P, NLOAD])
        sc = sbuf(ctx, nc, "d_sc", [P, NT, NE])
        s4 = sbuf(ctx, nc, "d_s4", [P, NT, NE])
        ta = sbuf(ctx, nc, "d_ta", [P, NT * NE])
        tb = sbuf(ctx, nc, "d_tb", [P, NT * NE])
        hi = sbuf(ctx, nc, "d_hi", [P, NT * NG, 4])
        lo = sbuf(ctx, nc, "d_lo", [P, NT * NG, 4])
        hi2 = sbuf(ctx, nc, "d_hi2", [P, NT * NG, 2])
        lo2 = sbuf(ctx, nc, "d_lo2", [P, NT * NG, 2])
        gs = sbuf(ctx, nc, "d_gs", [P, NT, NG])
        gm = sbuf(ctx, nc, "d_gm", [P, NT, NG])
        m8 = sbuf(ctx, nc, "d_m8", [P, NT, 8])
        sel = sbuf(ctx, nc, "d_sel", [P, NT, NE])
        selb = sbuf(ctx, nc, "d_selb", [P, NT, NE], BF16)
        wsum = sbuf(ctx, nc, "d_wsum", [P, NT])
        nb = sbuf(ctx, nc, "d_nb", [P, 3, NE])
        slot_i = sbuf(ctx, nc, "d_slot_i", [P, NT * 8], I32)
        pos_i = sbuf(ctx, nc, "d_pos_i", [P, 2, NT * 8], I32)
        pos = sbuf(ctx, nc, "d_pos", [P, 2, NT * 8])
        be = sbuf(ctx, nc, "d_be", [P, 2])
        be_i = sbuf(ctx, nc, "d_be_i", [P, 2], I32)
        oh_p = sbuf(ctx, nc, "d_oh_p", [P, 4, P], FP16)
        oh_b = sbuf(ctx, nc, "d_oh_b", [P, 4, NLOAD], FP16)

        ps_cum = psum(ctx, nc, "d_ps_cum", [P, 2, 512])
        ps_tot = psum(ctx, nc, "d_ps_tot", [P, 512])
        ps_inv = psum(ctx, nc, "d_ps_inv", [P, 512])

        (const_in, step, sig_done, sel_ready, cum_ready, oh_ready, oh_used, be_ready, be_out,
         be_in, w_ready, w_out, zeroed, cleared) = sems(
            ctx, nc, *("d_" + s for s in (
                "const_in step sig_done sel_ready cum_ready oh_ready oh_used be_ready be_out "
                "be_in w_ready w_out zeroed cleared").split()))
        block = ctx.enter_context(nc.Block())

        @block.sync
        def _(sp):
            sp.dma_start(sums[:, :, :], t["sums"]).then_inc(const_in, 16)
            sp.dma_start(order[:, :, :, :].rearrange("p a g h -> p (a g h)"),
                         t["order"].partition_broadcast(P)).then_inc(const_in, 16)
            sp.dma_start(bias[:, :], t["router_bias"].partition_broadcast(P)).then_inc(const_in, 16)
            sp.dma_start(tok_id[:, :], t["tok_id"]).then_inc(const_in, 16)
            sp.dma_start(iota[:, :], t["iota"].partition_broadcast(P)).then_inc(const_in, 16)
            sp.dma_start(blk_id[:, :], t["blk_id"]).then_inc(const_in, 16)
            sp.dma_start(pad_id[:, :], t["pad_id"]).then_inc(const_in, 16)
            sp.wait_ge(zeroed, 1)
            for name in ("sums_a", "sums_b"):
                sp.dma_start(t[name][0:TOK].rearrange("(p a) d -> p (a d)", p=P), zeros[:, :])\
                  .then_inc(cleared, 16)
            sp.dma_start(t["rows"][TOK:TOK + P, :], zeros[:, 0:ROW]).then_inc(cleared, 16)
            sp.wait_ge(w_ready, 1)
            sp.dma_start(t["rows"][0:TOK, D:ROW].rearrange("(n p) e -> p n e", p=P), w[:, :, :])\
              .then_inc(w_out, 16)
            sp.wait_ge(be_ready, 1)
            sp.dma_start(t["blocks"].rearrange("(c p) -> p c", p=P), be_i[:, :],
                         allow_slow_non_contiguous=True).then_inc(be_out, 16)
            sp.dma_start(t["blocks_f"].rearrange("(c p) -> p c", p=P), be[:, :],
                         allow_slow_non_contiguous=True).then_inc(be_out, 16)
            sp.wait_ge(be_out, 32)
            sp.dma_start(block_expert[:, :], t["blocks"].rearrange("(a c) -> a c", a=1))\
              .then_inc(be_in, 16)
            sp.dma_start(expert_f[:, :], t["blocks_f"].partition_broadcast(P)).then_inc(be_in, 16)
            sp.wait_ge(be_in, 32)
            sp.wait_ge(w_out, 16)
            sp.wait_ge(cleared, 48)

        @block.gpsimd
        def _(pool):
            pool.memset(zeros[:, :], 0.0).then_inc(zeroed, 1)

        @block.scalar
        def _(act):
            nc.scalar.activation(sc[:, :, :], logits[:, :, :], ACT.Sigmoid).then_inc(sig_done, 1)

        @block.vector
        def _(dve):
            ch = Chain(dve, step)
            V = nc.vector

            def tt(out, a, b, op):
                ch.step(V.tensor_tensor(out, a, b, op))

            dve.wait_ge(const_in, 7 * 16)
            dve.wait_ge(sig_done, 1)
            bc = bias[:, :].rearrange("p (a e) -> p a e", a=1).to_broadcast([P, NT, NE])
            tt(s4[:, :, :], sc[:, :, :], bc, ALU.add)
            v = s4[:, :, :].rearrange("p n (g c) -> p (n g) c", c=EPG)
            tt(hi[:, :, :], v[:, :, 0:4], v[:, :, 4:8], ALU.max)
            tt(lo[:, :, :], v[:, :, 0:4], v[:, :, 4:8], ALU.min)
            tt(hi2[:, :, :], hi[:, :, 0:2], hi[:, :, 2:4], ALU.max)
            tt(hi[:, :, 0:2], hi[:, :, 0:2], hi[:, :, 2:4], ALU.min)
            tt(lo[:, :, 0:2], lo[:, :, 0:2], lo[:, :, 2:4], ALU.max)
            tt(lo2[:, :, :], hi[:, :, 0:2], lo[:, :, 0:2], ALU.max)
            tt(hi[:, :, 0], hi2[:, :, 0], hi2[:, :, 1], ALU.max)
            tt(hi[:, :, 1], hi2[:, :, 0], hi2[:, :, 1], ALU.min)
            tt(lo[:, :, 0], lo2[:, :, 0], lo2[:, :, 1], ALU.max)
            tt(lo[:, :, 1], hi[:, :, 1], lo[:, :, 0], ALU.max)
            tt(gs[:, :, :].rearrange("p n g -> p (n g)"), hi[:, :, 0], lo[:, :, 1], ALU.add)
            gg = [P, NT * NG, NG]
            mine = gs[:, :, :].rearrange("p n (g a) -> p (n g) a", a=1).to_broadcast(gg)
            for i in range(NT):
                sl = slice(i * NG, (i + 1) * NG)
                others = gs[:, i:i + 1, :].to_broadcast([P, NG, NG])
                a = ta[:, :].rearrange("p (x h) -> p x h", h=NG)[:, sl]
                b = tb[:, :].rearrange("p (x h) -> p x h", h=NG)[:, sl]
                ch.did(V.tensor_tensor(a, others, mine[:, sl], ALU.is_ge))
                ch.did(V.tensor_tensor(b, others, mine[:, sl], ALU.is_gt))
            ch.last()
            for x, y in ((ta, 0), (tb, 1)):
                x4 = x[:, :].rearrange("p (n g) -> p n g", g=NG * NG)
                o = order[:, y:y + 1].rearrange("p a g h -> p a (g h)").to_broadcast([P, NT, NG * NG])
                tt(x4, x4, o, ALU.mult)
            tt(ta[:, :], ta[:, :], tb[:, :], ALU.add)
            ch.step(V.tensor_reduce(gm[:, :, :].rearrange("p n g -> p (n g)"),
                                    ta[:, :].rearrange("p (x h) -> p x h", h=NG), AX.X, ALU.add))
            ch.step(V.tensor_scalar(gm[:, :, :], gm[:, :, :], float(TOPG), None, ALU.is_lt))
            tmp = ta[:, :].rearrange("p (n e) -> p n e", e=NE)
            tt(ta[:, :].rearrange("p (x c) -> p x c", c=EPG), v,
               gm[:, :, :].rearrange("p n (g a) -> p (n g) a", a=1).to_broadcast([P, NT * NG, EPG]),
               ALU.mult)
            ch.step(V.tensor_scalar(ta[:, :], ta[:, :], 0.0, None, ALU.add))
            rep = tb[:, :].rearrange("p (n e) -> p n e", e=NE)
            for i in range(NT):
                ch.did(V.max(m8[:, i, :], tmp[:, i, :]))
            ch.last()
            for i in range(NT):
                ch.did(V.match_replace(rep[:, i, :], m8[:, i, :], tmp[:, i, :], -3e38))
            ch.last()
            tt(sel[:, :, :], tmp, rep, ALU.not_equal)
            V.tensor_copy(selb[:, :, :], sel[:, :, :]).then_inc(sel_ready, 1)
            tt(w[:, :, :], sc[:, :, :], sel[:, :, :], ALU.mult)
            ch.step(V.tensor_reduce(wsum[:, :], w[:, :, :], AX.X, ALU.add))
            ch.step(V.tensor_scalar(wsum[:, :], wsum[:, :], 1e-20, None, ALU.add))
            ch.step(V.reciprocal(wsum[:, :], wsum[:, :]))
            ch.step(V.tensor_scalar(wsum[:, :], wsum[:, :], RSCALE, None, ALU.mult))
            V.tensor_tensor(w[:, :, :], w[:, :, :],
                            wsum[:, :].rearrange("p (n a) -> p n a", a=1).to_broadcast([P, NT, NE]),
                            ALU.mult).then_inc(w_ready, 1)
            dve.wait_ge(cum_ready, 1)
            ch.step(V.tensor_scalar(nb[:, 0, :], ps_tot[:, 0:NE], (P - 1) / 2, 1.0 / P, ALU.add, ALU.mult))
            ch.step(V.tensor_scalar(nb[:, 0, :], nb[:, 0, :], 2.0 ** 23, None, ALU.add))
            ch.step(V.tensor_scalar(nb[:, 0, :], nb[:, 0, :], -2.0 ** 23, None, ALU.add))
            src = 0
            for k in range(6):
                a, b = nb[:, src, :], nb[:, 1 + k % 2, :]
                ch.did(V.tensor_copy(b[:, 0:1 << k], a[:, 0:1 << k]))
                tt(b[:, 1 << k:NE], a[:, 1 << k:NE], a[:, 0:NE - (1 << k)], ALU.add)
                src = 1 + k % 2
            incl, base = nb[:, src, :], nb[:, 3 - src, :]
            for c in range(2):
                tt(ta[:, c * NE:(c + 1) * NE], incl, blk_id[:, c:c + 1].to_broadcast([P, NE]), ALU.is_le)
            ch.step(V.tensor_reduce(be[:, :], ta[:, 0:2 * NE].rearrange("p (c e) -> p c e", c=2),
                                    AX.X, ALU.add))
            ch.step(V.tensor_scalar(be[:, :], be[:, :], NE - 1.0, None, ALU.min))
            V.tensor_copy(be_i[:, :], be[:, :]).then_inc(be_ready, 1)
            tt(base, incl, nb[:, 0, :], ALU.subtract)
            ch.step(V.tensor_scalar(base, base, float(P), 1.0, ALU.mult, ALU.add))
            tt(val[:, :, :], ps_cum[:, :, :].rearrange("p a (n e) -> p (a n) e", e=NE),
               base.rearrange("p (a e) -> p a e", a=1).to_broadcast([P, NT, NE]), ALU.add)
            tt(val[:, :, :], val[:, :, :], sel[:, :, :], ALU.mult)
            for i in range(NT):
                ch.did(V.max(v8[:, i, :], val[:, i, :]))
            ch.last()
            ch.step(V.tensor_scalar(slot_i[:, :], v8[:, :, :].rearrange("p n k -> p (n k)"),
                                    -1.0, None, ALU.add))
            ch.did(V.tensor_scalar(pos_i[:, 0, :], slot_i[:, :], P - 1, None, ALU.bitwise_and))
            ch.step(V.tensor_scalar(pos_i[:, 1, :], slot_i[:, :], 7, None, ALU.logical_shift_right))
            ch.step(V.tensor_copy(pos[:, :, :], pos_i[:, :, :]))
            for j in range(NT * 8):
                if j >= 4:
                    dve.wait_ge(oh_used, j - 3)
                V.tensor_scalar(oh_p[:, j % 4, :], iota[:, 0:P], pos[:, 0, j:j + 1],
                                tok_id[:, j // 8:j // 8 + 1], ALU.is_equal, ALU.mult).then_inc(oh_ready, 1)
                V.tensor_scalar(oh_b[:, j % 4, :], iota[:, :], pos[:, 1, j:j + 1], None,
                                ALU.is_equal).then_inc(oh_ready, 1)
            dve.wait_ge(oh_used, NT * 8)
            ch.step(V.tensor_scalar(is_pad[:, :], ps_inv[:, 0:NLOAD], 0.0, pad_id[:, :],
                                    ALU.is_equal, ALU.mult))
            ch.step(V.scalar_tensor_tensor(inv[:, :], ps_inv[:, 0:NLOAD], -1.0, is_pad[:, :],
                                           ALU.add, ALU.add))

        @block.tensor
        def _(pe):
            pe.wait_ge(const_in, 7 * 16)
            pe.wait_ge(sel_ready, 1)
            half = NT // 2
            for a in range(2):
                nc.tensor.matmul(ps_cum[:, a, :], sums[:, 0, :],
                                 selb[:, a * half:(a + 1) * half, :].rearrange("p n e -> p (n e)"),
                                 start=True, stop=False, skip_group_check=True)
                last = (a + 1) * half - 1
                for i in range(last):
                    first = max(a * half, i + 1)
                    n = last + 1 - first
                    nc.tensor.matmul(ps_cum[:, a, (first - a * half) * NE:512].rearrange(
                                         "p (n e) -> p n e", e=NE),
                                     sums[:, 1, :], selb[:, i:i + 1, :].to_broadcast([P, n, NE]),
                                     start=False, stop=(i == last - 1), skip_group_check=True)
            for i in range(NT):
                ins = nc.tensor.matmul(ps_tot[:, 0:NE], sums[:, 1, :], selb[:, i, :],
                                       start=(i == 0), stop=(i == NT - 1))
            ins.then_inc(cum_ready, 1)
            for j in range(NT * 8):
                pe.wait_ge(oh_ready, 2 * (j + 1))
                nc.tensor.matmul(ps_inv[:, 0:NLOAD], oh_p[:, j % 4, :], oh_b[:, j % 4, :],
                                 start=(j == 0), stop=(j == NT * 8 - 1)).then_inc(oh_used, 1)


def layer1_experts(nc, t, x_sb, qkv1, block_expert, expert_f, inv):
    ctx = ExitStack()
    with ctx:
        NS, NI = 4, 8
        ident = sbuf(ctx, nc, "e_ident", [P, P])
        iota = sbuf(ctx, nc, "e_iota", [P, NE])
        w_o = sbuf(ctx, nc, "e_w_o", [P, KD, D])
        w_gu = sbuf(ctx, nc, "e_w_gu", [P, NS, 2, KD, INTER1])
        w_d = sbuf(ctx, nc, "e_w_d", [HI1, NS, 2, D])
        idx = sbuf(ctx, nc, "e_idx", [P, NI], U32)
        x = sbuf(ctx, nc, "e_x", [P, NS, ROW])
        xT = sbuf(ctx, nc, "e_xT", [P, KD, P])
        pick = sbuf(ctx, nc, "e_pick", [P, NE])
        weight = sbuf(ctx, nc, "e_weight", [P, 2])
        sg = sbuf(ctx, nc, "e_sg", [P, INTER1])
        h = sbuf(ctx, nc, "e_h", [P, INTER1])
        hT = sbuf(ctx, nc, "e_hT", [HI1, 2, P])
        y = sbuf(ctx, nc, "e_y", [P, 2, D])
        prod = sbuf(ctx, nc, "e_prod", [P, B, D])
        s1 = sbuf(ctx, nc, "e_s1", [P, B, H1])
        e1 = sbuf(ctx, nc, "e_e1", [P, B, H1])
        mx = sbuf(ctx, nc, "e_mx", [P, H1])
        y1 = sbuf(ctx, nc, "e_y1", [P, D])
        yT = sbuf(ctx, nc, "e_yT", [P, KD, P])

        ps_xT = psum(ctx, nc, "e_ps_xT", [P, 512])
        ps_gu = psum(ctx, nc, "e_ps_gu", [P, 2, 512])
        ps_hT = psum(ctx, nc, "e_ps_hT", [P, 512])
        ps_y = psum(ctx, nc, "e_ps_y", [P, 512])
        ps_yT = psum(ctx, nc, "e_ps_yT", [P, 512])
        ps_o = psum(ctx, nc, "e_ps_o", [P, 512])

        (const_in, idx_ready, xT_ready, xT_copied, weighed, gu_ready, silu_ready, h_ready, hT_ready,
         hT_copied, y_ready, y_copied, waits, step, s_ready, e_ready, y1_ready, yT_ready,
         yT_copied, o_ready, cleared) = sems(
            ctx, nc, *("e_" + s for s in (
                "const_in idx_ready xT_ready xT_copied weighed gu_ready silu_ready h_ready hT_ready "
                "hT_copied y_ready y_copied waits step s_ready e_ready y1_ready yT_ready "
                "yT_copied o_ready cleared").split()))
        gu_in, d_in, x_in = (sems(ctx, nc, *(f"e_{s}{i}" for i in range(NS)))
                             for s in ("gu_in", "d_in", "x_in"))
        added = sems(ctx, nc, "e_added0", "e_added1")
        block = ctx.enter_context(nc.Block())
        BPQ = BPN // B

        def steps(eng, body):
            with eng.Fori(0, TPB) as n:
                for c in range(1, BPN + 1):
                    body(n, n * BPN + c, c)

        def use(n, c, of):
            return n * (BPN // of) + c // of

        @block.sync
        def _(sp):
            sp.dma_start(ident[:, :], t["ident"]).then_inc(const_in, 16)
            sp.dma_start(iota[:, :], t["iota_f"].partition_broadcast(P)).then_inc(const_in, 16)
            sp.dma_start(w_o[:, :, :], t["wo1T"].rearrange("(k p) i -> p k i", p=P))\
              .then_inc(const_in, 16)

            def load(j, s, free):
                e = sp.value_load(block_expert[0:1, bass.ds(j, 1)], min_val=0, max_val=NE - 1)
                if free:
                    sp.wait_ge(gu_ready, j - (NS - 1))
                for m, name in enumerate(("e_gate", "e_up")):
                    sp.dma_start(w_gu[:, s, m],
                                 t[name][bass.ds(e, 1)].rearrange("a p k i -> p (a k) i"))\
                      .then_inc(gu_in[s], 16)
                if free:
                    sp.wait_ge(y_ready, 1 + j - (NS - 1))
                sp.dma_start(w_d[:, s],
                             t["e_down"][bass.ds(e, 1)].rearrange("a p k d -> p (a k) d"))\
                  .then_inc(d_in[s], 16)

            for j in range(NS):
                load(j, j, False)
            with sp.Fori(1, NLOAD // NS) as i:
                for c in range(NS):
                    load(i * NS + c, c, True)
            for s in range(NS):
                sp.wait_ge(gu_in[s], NLOAD // NS * 32)
                sp.wait_ge(d_in[s], NLOAD // NS * 16)

        @block.gpsimd
        def _(pool):
            pool.memset(y[:, 0, :], 0.0).then_inc(cleared, 1)
            pool.wait_ge(cleared, 1)
            for a in range(2):
                pool.dma_start(t[("sums_a", "sums_b")[a]][TOK:TOK + P, :], y[:, 0, :])\
                    .then_inc(added[a], 16)

            def gather(j, c):
                nc.gpsimd.tensor_copy(idx[:, c % NI:c % NI + 1], inv[:, bass.ds(j, 1)])\
                  .then_inc(idx_ready, 1)
                pool.wait_ge(idx_ready, j + 1)
                apart(pool, waits)
                pool.indirect_dma_start(x[:, c % NS, :], None, t["rows"],
                                        bass.IndirectOffsetOnAxis(idx[:, c % NI:c % NI + 1], 0))\
                    .then_inc(x_in[c % NS], 16)

            for j in range(NS):
                gather(j, j)

            def step(n, j, c):
                pool.wait_ge(xT_ready, j)
                pool.wait_ge(weighed, j)
                gather(j + NS - 1, c + NS - 1)
                a = (c - 1) % 2
                pool.wait_ge(y_copied, 1 + j)
                pool.wait_ge(added[a], 16 + use(n, c - 1, 2) * 16)
                apart(pool, waits)
                pool.indirect_dma_start(t[("sums_a", "sums_b")[a]],
                                        bass.IndirectOffsetOnAxis(idx[:, (c - 1) % NI:(c - 1) % NI + 1], 0),
                                        y[:, a, :], None, compute_op=ALU.add).then_inc(added[a], 16)

            steps(pool, step)
            for a in range(2):
                pool.wait_ge(added[a], 16 + NBLK // 2 * 16)
            for s in range(NS):
                pool.wait_ge(x_in[s], NLOAD // NS * 16)

        @block.scalar
        def _(act):
            prime(act, y_copied)

            def silu(j, c):
                act.wait_ge(gu_ready, j + 1)
                act.wait_ge(h_ready, j)
                nc.scalar.activation(sg[:, :], ps_gu[:, c % 2, 0:INTER1], ACT.Silu)\
                  .then_inc(silu_ready, 1)

            silu(0, 0)

            def step(n, j, c):
                l, k = (c - 1) // BPQ, (c - 1) % BPQ
                if k == 10:
                    act.wait_ge(yT_ready, n * B + l + 1)
                    nc.scalar.activation(yT[:, :, :], ps_yT[:, 0:D].rearrange("p (k c) -> p k c", k=KD),
                                         ACT.Copy).then_inc(yT_copied, 1)
                silu(j, c)
                a = (c - 1) % 2
                act.wait_ge(y_ready, 1 + j)
                act.wait_ge(weighed, j)
                act.wait_ge(added[a], 16 + use(n, c - 1, 2) * 16)
                nc.scalar.activation(y[:, a, :], ps_y[:, 0:D], ACT.Copy, scale=weight[:, a:a + 1])\
                  .then_inc(y_copied, 1)
                if k == 5:
                    act.wait_ge(s_ready, n * B + l + 1)
                    nc.scalar.activation(e1[:, 0:l + 1, :], s1[:, 0:l + 1, :], ACT.Exp,
                                         scale=SCALE1).then_inc(e_ready, 1)

            steps(act, step)

        @block.vector
        def _(dve):
            prime(dve, hT_copied)
            V = nc.vector
            ch = Chain(dve, step)

            def copy_x(j, c):
                dve.wait_ge(xT_ready, j + 1)
                V.tensor_copy(xT[:, :, :].rearrange("p k c -> p (k c)"), ps_xT[:, 0:D])\
                 .then_inc(xT_copied, 1)

            def weigh(j, c):
                V.scalar_tensor_tensor(pick[:, :], iota[:, :], expert_f[:, bass.ds(j, 1)],
                                       x[:, c % NS, D:ROW], ALU.is_equal, ALU.mult,
                                       accum_out=weight[:, c % 2:c % 2 + 1]).then_inc(weighed, 1)

            def gate(j, c):
                dve.wait_ge(silu_ready, j + 1)
                dve.wait_ge(hT_ready, j)
                V.tensor_tensor(h[:, :], sg[:, :], ps_gu[:, c % 2, INTER1:2 * INTER1],
                                ALU.mult).then_inc(h_ready, 1)

            def copy_h(j):
                dve.wait_ge(hT_ready, j + 1)
                dve.wait_ge(y_ready, 1 + j)
                V.tensor_copy(hT[:, :, :].rearrange("p k c -> p (k c)"), ps_hT[0:HI1, 0:2 * P])\
                 .then_inc(hT_copied, 1)

            def attention(n, l, k):
                i = n * B + l
                m = l + 1

                def cols(a, b, c):
                    x4 = qkv1[:, :, c * D:(c + 1) * D].rearrange("p (l n) d -> p l n d", n=TPB)
                    return x4[:, a:b, bass.ds(n, 1), :].rearrange("p l n d -> p l (n d)")

                if k == 0:
                    ch.step(V.tensor_tensor(prod[:, 0:m, :], cols(l, l + 1, 0).to_broadcast([P, m, D]),
                                            cols(0, m, 1), ALU.mult))
                if k == 1:
                    ch.step(V.tensor_reduce(s1[:, 0:m, :].rearrange("p m h -> p (m h)"),
                                            prod[:, 0:m, :].rearrange("p m (h d) -> p (m h) d", d=DH1),
                                            AX.X, ALU.add))
                if k == 3:
                    ch.step(V.tensor_reduce(mx[:, :], s1[:, 0:m, :].rearrange("p m h -> p h m"),
                                            AX.X, ALU.max))
                    V.tensor_tensor(s1[:, 0:m, :], s1[:, 0:m, :],
                                    mx[:, :].rearrange("p (a h) -> p a h", a=1).to_broadcast([P, m, H1]),
                                    ALU.subtract).then_inc(s_ready, 1)
                if k == 6:
                    dve.wait_ge(e_ready, i + 1)
                    ch.step(V.tensor_reduce(mx[:, :], e1[:, 0:m, :].rearrange("p m h -> p h m"),
                                            AX.X, ALU.add))
                    ch.step(V.reciprocal(mx[:, :], mx[:, :]))
                    ch.step(V.tensor_tensor(e1[:, 0:m, :], e1[:, 0:m, :],
                                            mx[:, :].rearrange("p (a h) -> p a h", a=1)
                                            .to_broadcast([P, m, H1]), ALU.mult))
                if k == 7:
                    ch.step(V.tensor_tensor(
                        prod[:, 0:m, :].rearrange("p m (h d) -> p (m h) d", d=DH1),
                        cols(0, m, 2).rearrange("p m (h d) -> p m h d", d=DH1),
                        e1[:, 0:m, :].rearrange("p m (h a) -> p m h a", a=1)
                        .to_broadcast([P, m, H1, DH1]), ALU.mult))
                if k == 8:
                    V.tensor_reduce(y1[:, :], prod[:, 0:m, :].rearrange("p m d -> p d m"),
                                    AX.X, ALU.add).then_inc(y1_ready, 1)
                if k == 11:
                    dve.wait_ge(o_ready, i + 1)
                    o = x_sb[:, :, :].rearrange("p (l n) d -> p l n d", n=TPB)
                    o = o[:, l, bass.ds(n, 1), :].rearrange("p n d -> p (n d)")
                    ch.step(V.tensor_tensor(o, o, ps_o[:, 0:D], ALU.add))

            copy_x(0, 0)
            weigh(0, 0)
            gate(0, 0)
            copy_x(1, 1)
            PER = B * 8

            with dve.Fori(0, TPB) as n:
                ch.enter(n, PER)
                for c in range(1, BPN + 1):
                    j = n * BPN + c
                    copy_h(j - 1)
                    gate(j, c)
                    copy_x(j + 1, c + 1)
                    dve.wait_ge(weighed, j)
                    dve.wait_ge(y_copied, 1 + j - 1)
                    weigh(j, c)
                    attention(n, (c - 1) // BPQ, (c - 1) % BPQ)
                ch.leave(TPB, PER)

        @block.tensor
        def _(pe):
            prime(pe, y_ready)
            pe.wait_ge(const_in, 48)

            def transpose_x(n, j, c):
                pe.wait_ge(x_in[c % NS], (use(n, c, NS) + 1) * 16)
                pe.wait_ge(xT_copied, j)
                for k in range(KD):
                    ins = nc.tensor.transpose(ps_xT[:, k * P:(k + 1) * P],
                                              x[:, c % NS, k * P:(k + 1) * P], ident[:, :])
                ins.then_inc(xT_ready, 1)

            def gate_up(n, j, c):
                pe.wait_ge(xT_copied, j + 1)
                pe.wait_ge(gu_in[c % NS], (use(n, c, NS) + 1) * 32)
                for k in range(KD):
                    ins = nc.tensor.matmul(
                        ps_gu[:, c % 2, 0:2 * INTER1].rearrange("p (m i) -> p m i", m=2),
                        xT[:, k, :], w_gu[:, c % NS, :, k, :], start=(k == 0), stop=(k == KD - 1))
                ins.then_inc(gu_ready, 1)

            def transpose_h(j):
                pe.wait_ge(h_ready, j + 1)
                pe.wait_ge(hT_copied, 1 + j)
                for k in range(2):
                    ins = nc.tensor.transpose(ps_hT[0:HI1, k * P:(k + 1) * P],
                                              h[:, k * HI1:(k + 1) * HI1], ident[:, :])
                ins.then_inc(hT_ready, 1)

            def down(n, j, c):
                pe.wait_ge(hT_copied, 1 + j + 1)
                pe.wait_ge(d_in[c % NS], (use(n, c, NS) + 1) * 16)
                pe.wait_ge(y_copied, 1 + j)
                for k in range(2):
                    ins = nc.tensor.matmul(ps_y[:, 0:D], hT[:, k, :], w_d[:, c % NS, k, :],
                                           start=(k == 0), stop=(k == 1))
                ins.then_inc(y_ready, 1)

            transpose_x(0, 0, 0)
            gate_up(0, 0, 0)
            transpose_x(0, 1, 1)

            def step(n, j, c):
                transpose_h(j - 1)
                gate_up(n, j, c)
                transpose_x(n, j + 1, c + 1)
                down(n, j - 1, c - 1)
                l, k = (c - 1) // BPQ, (c - 1) % BPQ
                if k == 9:
                    pe.wait_ge(y1_ready, n * B + l + 1)
                    for a in range(KD):
                        ins = nc.tensor.transpose(ps_yT[:, a * P:(a + 1) * P],
                                                  y1[:, a * P:(a + 1) * P], ident[:, :])
                    ins.then_inc(yT_ready, 1)
                if k == 10:
                    pe.wait_ge(yT_copied, n * B + l + 1)
                    for a in range(KD):
                        ins = nc.tensor.matmul(ps_o[:, 0:D], yT[:, a, :], w_o[:, a, :],
                                               start=(a == 0), stop=(a == KD - 1))
                    ins.then_inc(o_ready, 1)

            steps(pe, step)


def layer1_combine(nc, t, x_sb):
    ctx = ExitStack()
    with ctx:
        sums = [sbuf(ctx, nc, f"f_sums_{s}", [P, NT, D]) for s in "ab"]
        step, ready, stored = sems(ctx, nc, "f_step", "f_ready", "f_stored")
        sums_in = sems(ctx, nc, *(f"f_sums_in{b}" for b in range(B)))
        block = ctx.enter_context(nc.Block())

        def part(x, b):
            return x[b * T:(b + 1) * T, :].rearrange("(i p) d -> p i d", p=P)

        @block.sync
        def _(sp):
            for b in range(B):
                for x, name in zip(sums, ("sums_a", "sums_b")):
                    sp.dma_start(x[:, b * TPB:(b + 1) * TPB, :], part(t[name], b))\
                      .then_inc(sums_in[b], 16)
            for b in range(B):
                sp.wait_ge(ready, b + 1)
                sp.dma_start(part(t["out"], b), sums[0][:, b * TPB:(b + 1) * TPB, :])\
                  .then_inc(stored, 16)
            sp.wait_ge(stored, B * 16)

        @block.vector
        def _(dve):
            for b in range(B):
                a = slice(b * TPB, (b + 1) * TPB)
                dve.wait_ge(sums_in[b], 32)
                nc.vector.tensor_tensor(sums[0][:, a, :], sums[0][:, a, :], sums[1][:, a, :], ALU.add)\
                  .then_inc(step, 1)
                dve.wait_ge(step, b + 1)
                nc.vector.tensor_tensor(sums[0][:, a, :], sums[0][:, a, :], x_sb[:, a, :], ALU.add)\
                  .then_inc(ready, 1)


def kernel_program(nc, t):
    ctx = ExitStack()
    with ctx:
        x_sb = sbuf(ctx, nc, "x_sb", [P, NT, D])
        yn = sbuf(ctx, nc, "yn", [P, NT, D])
        with nc.sbuf_tensor("v_pad", [P, NT, HKV, VW], F32) as v_pad:
            layer0_dense(nc, t, x_sb, v_pad)
            layer0_attention(nc, t, v_pad, yn)
        qkv1 = sbuf(ctx, nc, "qkv1", [P, NT, 3 * D])
        inv = sbuf(ctx, nc, "inv", [P, NLOAD], U32)
        block_expert = sbuf(ctx, nc, "block_expert", [1, 2 * P], I32)
        expert_f = sbuf(ctx, nc, "expert_f", [P, 2 * P])
        with nc.sbuf_tensor("logits", [P, NT, NE], F32) as logits:
            layer1_front(nc, t, x_sb, yn, qkv1, logits)
            layer1_routing(nc, t, logits, block_expert, expert_f, inv)
        layer1_experts(nc, t, x_sb, qkv1, block_expert, expert_f, inv)
        layer1_combine(nc, t, x_sb)


def constants():
    c = {}
    h = np.array([[1.0]])
    while h.shape[0] < P:
        h = np.block([[h, h], [h, -h]])
    c["had"] = np.stack([h / 16, -h / 16, h / 32], axis=1).astype(np.float32)
    c["ident"] = np.eye(P, dtype=np.float32)
    causal = np.where(np.arange(P)[None, :] > np.arange(P)[:, None], -3e38, 0.0)
    c["mask"] = np.concatenate([np.zeros((P, T - P)), causal], axis=1).astype(np.float32)
    c["causal"] = causal.T.astype(np.dtype("bfloat16"))
    before = np.arange(P)[:, None] < np.arange(P)[None, :]
    c["sums"] = np.stack([before, np.ones((P, P))], axis=1).astype(np.dtype("bfloat16"))
    g = np.arange(NG)
    c["order"] = np.stack([g[None, :] < g[:, None], g[None, :] > g[:, None]])\
        .astype(np.float32).reshape(-1)
    c["tok_id"] = (1 + np.arange(P)[:, None] + P * np.arange(NT)[None, :]).astype(np.float32)
    c["pad_id"] = (1 + TOK + np.arange(P)[:, None]).astype(np.float32)
    c["iota_f"] = np.arange(NE).astype(np.float32)
    c["blk_id"] = (np.arange(P)[:, None] + P * np.arange(2)[None, :]).astype(np.float32)
    c["iota"] = np.arange(NLOAD).astype(np.float16)
    pad = np.zeros((2, SROWS - MROW, T))
    pad[1, 0:NP_] = 1.0
    c["pad"] = pad.astype(np.dtype("bfloat16"))
    c["identb"] = np.eye(P).astype(np.dtype("bfloat16"))
    theta = (1.0 / 10000.0 ** (np.arange(0, HD, 2, dtype=np.float32) / HD)).astype(np.float32)
    freqs = np.arange(T, dtype=np.float32)[:, None] * theta[None, :]
    cos = np.repeat(np.cos(freqs), 2, axis=1)
    sin = np.stack([-np.sin(freqs), np.sin(freqs)], axis=-1).reshape(T, HD)
    c["rope"] = np.stack([cos, sin], axis=1).astype(np.float32).reshape(TPB, P, 2, HD)\
        .transpose(1, 0, 2, 3)
    return c


def kernel(**inputs):
    import numpy as _np
    import concourse.bacc as _bacc
    from concourse import mybir as _mybir
    from concourse.bass_utils import run_bass_kernel_spmd as _run

    a = {k: _np.asarray(v) for k, v in inputs.items()}
    given = constants()
    given["x"] = a["L0_attn_x"].reshape(TOK, D)
    for name, key in (("wqT", "L0_attn_wq"), ("wkT", "L0_attn_wk"), ("wvT", "L0_attn_wv"),
                      ("woT", "L0_attn_wo"), ("w_upT", "L0_ffn_W_up"), ("w_gateT", "L0_ffn_W_gate"),
                      ("w_downT", "L0_ffn_W_down"), ("w_qkv1T", "L1_attn_weight_qkv"),
                      ("wo1T", "L1_attn_weight_out"), ("routerT", "L1_ffn_gate_weight")):
        given[name] = a[key].T
    for name, key in (("su_ug", "L0_ffn_SU_ug"), ("su_dp", "L0_ffn_SU_dp"),
                      ("ws_ug", "L0_ffn_Wscale_ug"), ("ws_dp", "L0_ffn_Wscale_dp"),
                      ("router_bias", "L1_ffn_e_score_correction_bias")):
        given[name] = a[key]
    for name, key in (("e_gate", "L1_ffn_gate_proj"), ("e_up", "L1_ffn_up_proj")):
        given[name] = a[key].reshape(NE, INTER1, KD, P).transpose(0, 3, 2, 1)
    given["e_down"] = a["L1_ffn_down_proj"].reshape(NE, D, 2, HI1).transpose(0, 3, 2, 1)

    nc = _bacc.Bacc("TRN2", target_bir_lowering=False, num_devices=1)
    arrays, t = {}, {}
    for name, v in given.items():
        arrays[name] = _np.ascontiguousarray(v)
        t[name] = nc.dram_tensor(name, arrays[name].shape, _mybir.dt.from_np(arrays[name].dtype),
                                 kind="ExternalInput").ap()
    for name, (shape, dt) in SCRATCH.items():
        t[name] = nc.dram_tensor(name, shape, dt).ap()
    t["out"] = nc.dram_tensor("out", (TOK, D), F32, kind="ExternalOutput").ap()
    kernel_program(nc, t)
    r = _run(nc, [arrays], core_ids=[0])
    return r.results[0]["out"].reshape(B, T, D)
```
